# Optimizing a Trainium2 kernel written in Bass

```python
import numpy as np
import jax
import jax.numpy as jnp

def _softmax(x, axis=-1):
    return jax.nn.softmax(x, axis=axis)

def _gelu(x):
    return jax.nn.gelu(x, approximate=True)

def _silu(x):
    return jax.nn.silu(x)

def _sigmoid(x):
    return jax.nn.sigmoid(x)

def _layernorm(x, axis=-1, eps=1e-05):
    m = jnp.mean(x, axis=axis, keepdims=True)
    v = jnp.var(x, axis=axis, keepdims=True)
    return (x - m) / jnp.sqrt(v + eps)

def _scatter_add(tgt, idx, src, axis=0):
    return tgt.at[idx].add(src)

def _segment_sum(src, seg, n):
    return jax.ops.segment_sum(src, seg, n)
kernel_name = 'mk_gnn_preln_d2_gnn_r8_c7384d'

def setup_inputs(seed: int=0):
    np.random.seed(seed)
    _w = jnp.asarray

    def _rec_inputs():
        import jax
        import jax.numpy as jnp
        _gk = jax.random.key(seed)
        x = -0.0009044 + 1 * jax.random.normal(jax.random.fold_in(_gk, 1), (12500, 16), jnp.float32)
        _s = jax.random.randint(jax.random.fold_in(_gk, 2), (200000,), 0, 12500, jnp.int32)
        _d = jax.random.randint(jax.random.fold_in(_gk, 3), (200000,), 0, 12500, jnp.int32)
        _loop = jnp.arange(12500, dtype=jnp.int32)
        src = jnp.concatenate([_s, _d, _loop])
        dst = jnp.concatenate([_d, _s, _loop])
        _o = jnp.argsort(dst, stable=True)
        src = src[_o]
        dst = dst[_o]
        edge_attr_16 = 0.000254407 + 0.99978 * jax.random.normal(jax.random.fold_in(_gk, 11), (412500, 16), jnp.float32)
        edge_attr_8 = -5.3897e-05 + 0.999841 * jax.random.normal(jax.random.fold_in(_gk, 12), (412500, 8), jnp.float32)
        node_vec1 = -0.00472126 + 0.997171 * jax.random.normal(jax.random.fold_in(_gk, 14), (12500, 1), jnp.float32)
        return (x, src, dst, edge_attr_16, edge_attr_8, node_vec1)
    x, src, dst, edge_attr_16, edge_attr_8, node_vec1 = _rec_inputs()

    def _L0_gnn_setup():
        import jax, jax.numpy as jnp
        import numpy as np
        N_NODES = 12500
        N_EDGES = 62500
        IND = 16
        OUT = 16
        EDGE_DIM = 16
        HID = IND * OUT
        BN_EPS = 1e-05
        key = jax.random.key(seed)
        ks = jax.random.split(key, 12)
        x = jax.random.normal(ks[0], (N_NODES, IND), dtype=jnp.float32)
        edge_index = jax.random.randint(ks[1], (2, N_EDGES), 0, N_NODES, dtype=jnp.int64)
        edge_attr = jax.random.normal(ks[2], (N_EDGES, EDGE_DIM), dtype=jnp.float32)
        W1 = jax.random.normal(ks[3], (EDGE_DIM, HID), dtype=jnp.float32) * (1.0 / np.sqrt(EDGE_DIM))
        b1 = jnp.zeros((HID,), dtype=jnp.float32)
        W2 = jax.random.normal(ks[4], (HID, HID), dtype=jnp.float32) * (1.0 / np.sqrt(HID))
        b2 = jnp.zeros((HID,), dtype=jnp.float32)
        root = jax.random.normal(ks[5], (IND, OUT), dtype=jnp.float32) * (1.0 / np.sqrt(IND))
        bias = jnp.zeros((OUT,), dtype=jnp.float32)
        gamma = jnp.ones((OUT,), dtype=jnp.float32)
        beta = jnp.zeros((OUT,), dtype=jnp.float32)
        return {'x': x, 'edge_index': edge_index, 'edge_attr': edge_attr, 'W1': W1, 'b1': b1, 'W2': W2, 'b2': b2, 'root': root, 'bias': bias, 'gamma': gamma, 'beta': beta}
    _L0_gnn_all = _L0_gnn_setup()
    _L0_gnn_in = {k: v for k, v in _L0_gnn_all.items() if k in ('W1', 'b1', 'W2', 'b2', 'root', 'bias', 'gamma', 'beta')}
    del _L0_gnn_all

    def _L1_gnn_setup():
        import jax, jax.numpy as jnp
        import numpy as np
        N_NODES = 12500
        N_EDGES = 400000
        D_NODE = 16
        D_EDGE = 8
        D_HIDDEN = 16
        key = jax.random.key(seed)
        ks = jax.random.split(key, 8)
        node_features = jax.random.normal(ks[0], (N_NODES, D_NODE), dtype=jnp.float32)
        edge_attr_e3nn = jax.random.normal(ks[1], (N_EDGES, D_EDGE), dtype=jnp.float32)
        node_attr_scalar_raw = jax.random.normal(ks[2], (N_NODES, 1), dtype=jnp.float32)
        W_msg_tp = jax.random.normal(ks[3], (D_NODE, D_EDGE, D_HIDDEN), dtype=jnp.float32)
        W_msg_lin = jax.random.normal(ks[4], (D_HIDDEN, D_HIDDEN), dtype=jnp.float32)
        W_upd_tp = jax.random.normal(ks[5], (D_NODE, D_HIDDEN, D_HIDDEN), dtype=jnp.float32)
        W_upd_lin = jax.random.normal(ks[6], (D_HIDDEN, D_NODE), dtype=jnp.float32)
        edge_index = jax.random.randint(ks[7], (2, N_EDGES), 0, N_NODES, dtype=jnp.int64)
        return {'node_features': node_features, 'edge_attr_e3nn': edge_attr_e3nn, 'node_attr_scalar_raw': node_attr_scalar_raw, 'W_msg_tp': W_msg_tp, 'W_msg_lin': W_msg_lin, 'W_upd_tp': W_upd_tp, 'W_upd_lin': W_upd_lin, 'edge_index': edge_index}
    _L1_gnn_all = _L1_gnn_setup()
    _L1_gnn_in = {k: v for k, v in _L1_gnn_all.items() if k in ('W_msg_tp', 'W_msg_lin', 'W_upd_tp', 'W_upd_lin')}
    del _L1_gnn_all
    return {'x': x, 'src': src, 'dst': dst, 'edge_attr_16': edge_attr_16, 'edge_attr_8': edge_attr_8, 'node_vec1': node_vec1, 'L0_gnn_W1': _L0_gnn_in['W1'], 'L0_gnn_b1': _L0_gnn_in['b1'], 'L0_gnn_W2': _L0_gnn_in['W2'], 'L0_gnn_b2': _L0_gnn_in['b2'], 'L0_gnn_root': _L0_gnn_in['root'], 'L0_gnn_bias': _L0_gnn_in['bias'], 'L0_gnn_gamma': _L0_gnn_in['gamma'], 'L0_gnn_beta': _L0_gnn_in['beta'], 'L1_gnn_W_msg_tp': _L1_gnn_in['W_msg_tp'], 'L1_gnn_W_msg_lin': _L1_gnn_in['W_msg_lin'], 'L1_gnn_W_upd_tp': _L1_gnn_in['W_upd_tp'], 'L1_gnn_W_upd_lin': _L1_gnn_in['W_upd_lin']}

def reference(x, src, dst, edge_attr_16, edge_attr_8, node_vec1, L0_gnn_W1, L0_gnn_b1, L0_gnn_W2, L0_gnn_b2, L0_gnn_root, L0_gnn_bias, L0_gnn_gamma, L0_gnn_beta, L1_gnn_W_msg_tp, L1_gnn_W_msg_lin, L1_gnn_W_upd_tp, L1_gnn_W_upd_lin):
    import jax
    import jax.numpy as jnp

    def _L0_gnn_ref(x, edge_index, edge_attr, W1, b1, W2, b2, root, bias, gamma, beta):
        import jax, jax.numpy as jnp
        import numpy as np
        N_NODES = 12500
        N_EDGES = 62500
        IND = 16
        OUT = 16
        EDGE_DIM = 16
        HID = IND * OUT
        BN_EPS = 1e-05
        n_nodes, ind = x.shape
        out_dim = root.shape[1]
        src, dst = (edge_index[0], edge_index[1])
        h = jax.nn.relu(edge_attr @ W1 + b1)
        w_edge = (h @ W2 + b2).reshape(-1, ind, out_dim)
        msgs = jnp.einsum('ei,eio->eo', x[src], w_edge)
        aggr = jax.ops.segment_sum(msgs, dst, num_segments=n_nodes)
        out = aggr + x @ root + bias
        mean = out.mean(axis=0)
        var = out.var(axis=0)
        out = (out - mean) / jnp.sqrt(var + BN_EPS) * gamma + beta
        return jax.nn.relu(out)

    def _L1_gnn_ref(node_features, edge_attr_e3nn, node_attr_scalar_raw, W_msg_tp, W_msg_lin, W_upd_tp, W_upd_lin, edge_index):
        import jax, jax.numpy as jnp
        import numpy as np
        N_NODES = 12500
        N_EDGES = 400000
        D_NODE = 16
        D_EDGE = 8
        D_HIDDEN = 16
        n_nodes = node_features.shape[0]
        row = edge_index[0]
        col = edge_index[1]
        norm_msg_tp = 1.0 / np.float32(np.sqrt(D_NODE * D_EDGE))
        norm_upd_tp = 1.0 / np.float32(np.sqrt(D_NODE * D_HIDDEN))
        norm_lin = 1.0 / np.float32(np.sqrt(D_HIDDEN))
        x_j = node_features[col]
        m = jnp.einsum('ei,ej,ijh->eh', x_j, edge_attr_e3nn, W_msg_tp) * norm_msg_tp
        m = jax.nn.silu(m)
        m = m @ W_msg_lin * norm_lin
        agg = jax.ops.segment_sum(m, row, num_segments=n_nodes)
        u = jnp.einsum('ni,nh,ihk->nk', node_features, agg, W_upd_tp) * norm_upd_tp
        u = jax.nn.silu(u)
        u = u @ W_upd_lin * norm_lin
        return node_features + u
    edge_index = jnp.stack([src, dst])
    h = jnp.maximum(_layernorm(x, axis=-1), 0.0)
    x = x + _L0_gnn_ref(h, edge_index, edge_attr_16, L0_gnn_W1, L0_gnn_b1, L0_gnn_W2, L0_gnn_b2, L0_gnn_root, L0_gnn_bias, L0_gnn_gamma, L0_gnn_beta)
    h = jnp.maximum(_layernorm(x, axis=-1), 0.0)
    x = x + _L1_gnn_ref(h, edge_attr_8, node_vec1, L1_gnn_W_msg_tp, L1_gnn_W_msg_lin, L1_gnn_W_upd_tp, L1_gnn_W_upd_lin, edge_index)
    return x

_drawn_inputs = setup_inputs


def setup_inputs(seed=0):
    import zlib

    import numpy as np

    out = dict(_drawn_inputs(seed))
    spreads = {'L0_gnn_b1': (0.0, 0.1),
     'L0_gnn_b2': (0.0, 0.1),
     'L0_gnn_bias': (0.0, 0.1),
     'L0_gnn_gamma': (1.0, 0.2),
     'L0_gnn_beta': (0.0, 0.1)}
    factors = {}
    for name, (base, spread) in spreads.items():
        noise = np.random.default_rng([zlib.crc32(name.encode()), seed]).standard_normal(out[name].shape)
        drawn = base * np.exp(spread * noise) if base else spread * noise
        out[name] = jnp.asarray(drawn.astype(out[name].dtype))
    for name, factor in factors.items():
        out[name] = (out[name] * factor).astype(out[name].dtype)
    return out
```

```python
import math
from contextlib import ExitStack, contextmanager

import numpy as np

import concourse.bass as bass
from concourse import mybir

P = 128
D = 16
T = 8
GE = P * T
W = 2
WIDE = 1
TP = T - WIDE
HI = P // D
LN_EPS = 1e-5
BN_EPS = 1e-5

f32, bf16 = mybir.dt.float32, mybir.dt.bfloat16
i32, i16 = mybir.dt.int32, mybir.dt.int16
ALU = mybir.AluOpType
ACT = mybir.ActivationFunctionType
X = mybir.AxisListType.X


def need(engine, sem, count):
    if isinstance(count, int) and count <= 0:
        return
    engine.wait_ge(sem, count)


def each(engine, count, body, head=2, tail=0):
    for c in range(head):
        body(c, c % 2, c // 2)
    assert (count - head - tail) % 2 == 0
    with engine.Fori(0, (count - head - tail) // 2) as i:
        for u in range(head, head + 2):
            body(i * 2 + u, u % 2, i + u // 2)
    for c in range(count - tail, count):
        body(c, c % 2, c // 2)


def chain(engine, sem):
    count = [0]

    def link(instruction):
        count[0] += 1
        instruction.then_inc(sem, 1)
        engine.wait_ge(sem, count[0])
    return link


def clear_all(nc, sems):
    nums = [s.num for s in sems]
    nc.all_engine_barrier(sems_to_clear=range(min(nums), max(nums) + 1))


@contextmanager
def semaphores(nc):
    held = []
    with ExitStack() as c:
        def sem(name):
            held.append(c.enter_context(nc.semaphore(name)))
            return held[-1]
        yield sem
        clear_all(nc, held)


class Shapes:
    def __init__(self, n, e):
        self.N, self.E = n, e
        self.FULL = e // GE
        self.G = 2 * math.ceil((self.FULL + 1) / 2)
        self.DUP = GE - e % GE
        assert self.FULL in (self.G - 1, self.G - 2) and self.G % 4 == 0
        self.CH = 4
        self.CG = self.G // self.CH
        assert self.CG <= P
        self.B = math.ceil(n / P)
        self.REST = n - P * (self.B - 1)
        self.NC = math.ceil((self.B + W) / T)
        self.BP = T * self.NC
        self.LC = math.ceil(math.ceil(n / HI) / 4)
        self.LO = math.ceil(n / HI)
        assert self.LC <= 512 and HI * self.LO <= n + P


def build(nc, x, src, dst, ea16, ea8, W1, b1, W2, b2, root, bias, gamma, beta,
          Wmsg, Wmsg_lin, Wupd, Wupd_lin, out):
    S = Shapes(x.shape[0], src.shape[0])
    with ExitStack() as ctx:
        def sb(name, shape, dt, c=ctx):
            return c.enter_context(nc.sbuf_tensor(name, shape, dt))

        class K:
            pass
        k = K()
        k.rows = nc.dram_tensor("gather_rows", (S.N, 2 * D), f32, kind="Internal").ap()
        k.dst_rows = nc.dram_tensor("dst_rows", (S.G, GE), i16, kind="Internal").ap()
        k.src_rows = nc.dram_tensor("src_rows", (S.G, GE), i16, kind="Internal").ap()
        k.sums = [nc.dram_tensor(f"sums{t}", (S.N + P, D), f32, kind="Internal").ap() for t in range(T)]
        k.sums_all = nc.dram_tensor("sums_all", (S.N, D), f32, kind="Internal").ap()

        k.ident = sb("ident", [P, P], f32)
        k.identb = sb("identb", [P, P], bf16)
        k.ones = sb("ones", [P, P], f32)
        k.pidx = sb("pidx", [P, 1], f32)
        k.trash = sb("trash", [P, 1], f32)
        k.weight = sb("weight", [P, 1], f32)
        k.weight25 = sb("weight25", [P, 1], f32)
        k.iota = sb("iota", [P, W * P], bf16)
        k.valid = sb("valid", [P, S.BP], f32)
        k.zeros = sb("zeros", [P, 512], f32)
        k.W1p = sb("W1p", [96, 256], bf16)
        k.b1 = sb("b1c", [P, 2], f32)
        k.W2 = sb("W2s", [P, 2, 256], f32)
        k.bias = sb("biasb", [P, D], f32)
        k.gamma = sb("gammab", [P, D], f32)
        k.beta = sb("betab", [P, D], f32)
        k.bd_pre = sb("bd_pre", [P, T, 2 * D], f32)
        k.bd_lin = sb("bd_lin", [P, T, D], f32)
        k.bd_out = sb("bd_out", [P, T, D], f32)
        k.x = sb("xn", [P, S.BP, D], f32)
        k.h = sb("hn", [P, S.BP, D], f32)
        k.agg = sb("aggn", [P, S.BP, D], f32)
        k.dst = sb("dst_t", [P, S.G, T], f32)
        k.src = sb("src_t", [P, S.G, T], f32)
        k.first = sb("first_t", [P, S.G], f32)
        k.base = sb("base_t", [P, S.G], f32)
        k.win = sb("win_t", [P, S.G], f32)
        k.win_i = sb("win_i", [1, S.G], i32)
        k.rel = sb("rel_t", [P, S.G, T], f32)
        k.passes = sb("passes", [P, 1], i32)

        with semaphores(nc) as sem:
            setup_indices(nc, S, k, sem, src, dst)
            setup_nodes(nc, S, k, sem, x, W1, b1, W2, b2, root, bias, gamma, beta,
                        Wmsg_lin, Wupd_lin)
        n_passes = nc.values_load(k.passes[0:1, 0:1], min_val=1, max_val=S.B // W + 1)

        with semaphores(nc) as sem, ExitStack() as c:
            pre_layer(nc, S, k, sem, c)
        with semaphores(nc) as sem, ExitStack() as c:
            layer0(nc, S, k, sem, c, ea16, n_passes)
        with ExitStack() as c:
            k.Q = sb("Q", [P, S.BP, 3, P], bf16, c)
            with semaphores(nc) as sem, ExitStack() as cc:
                between(nc, S, k, sem, cc, Wmsg)
            with semaphores(nc) as sem:
                layer1(nc, S, k, sem, c, ea8, n_passes)
        with semaphores(nc) as sem, ExitStack() as c:
            finish(nc, S, k, sem, c, Wupd, out)


def setup_indices(nc, S, k, sem, src, dst):
    CG, CH, G = S.CG, S.CH, S.G
    with ExitStack() as c:
        def sb(name, shape, dt):
            return c.enter_context(nc.sbuf_tensor(name, shape, dt))
        raw = [[sb(f"raw{w}{i}", [CG, GE], i32) for i in range(CH)] for w in "ds"]
        flt = [[sb(f"flt{w}{i}", [CG, GE], f32) for i in range(CH)] for w in "ds"]
        perm = [[sb(f"perm{w}{i}", [CG, T, P], i16) for i in range(CH)] for w in "ds"]
        lohi = sb("lohi", [CG, CH, 2], f32)
        lohi_i = sb("lohi_i", [CG, CH, 2], i32)
        blk = sb("blk", [CG, CH, 2], f32)
        qrep = sb("qrep", [CG, CH, 2, P], f32)
        span = sb("span", [P, G], f32)
        smax = sb("smax", [P, 2], f32)
        smax_i = sb("smax_i", [P, 2], i32)
        wint = sb("wint", [P, 1], i32)
        iota_i = sb("iota_i", [P, W * P], i32)
        pidx_i = sb("pidx_i", [P, 1], i32)
        ps_d = [c.enter_context(nc.psum_tensor(f"ps_d{i}", [P, 4, P], f32)) for i in range(2)]
        ps_s = [c.enter_context(nc.psum_tensor(f"ps_s{i}", [P, 4, P], f32)) for i in range(2)]
        ps_q = c.enter_context(nc.psum_tensor("ps_q", [P, 2, P], f32))

        idx_in = [sem(f"idx_in{i}") for i in range(CH)]
        rows_out = sem("rows_out")
        cst0, cst = sem("cst0"), sem("cst")
        dve = sem("ix_dve")
        reduced, masked = sem("reduced"), sem("masked")
        d_flt, s_flt = sem("d_flt"), sem("s_flt")
        d_perm, s_perm = sem("d_perm"), sem("s_perm")
        q_ready = sem("q_ready")
        tr_d, tr_s = sem("tr_d"), sem("tr_s")
        ev_d, ev_s = sem("ev_d"), sem("ev_s")

        block = c.enter_context(nc.Block())

        @block.sync
        def _(sp):
            for i in range(CH):
                for w, table in enumerate((dst, src)):
                    n = min(S.FULL, (i + 1) * CG) - i * CG
                    sp.dma_start(raw[w][i][0:n, :],
                                 table[i * CG * GE:(i * CG + n) * GE].rearrange("(g f) -> g f", f=GE)
                                 ).then_inc(idx_in[i], 16)
                    for r in range(n, CG):
                        sp.dma_start(raw[w][i][r:r + 1, :],
                                     table[S.E - GE:S.E].rearrange("(g f) -> g f", f=GE)
                                     ).then_inc(idx_in[i], 16)
            for i in range(CH):
                sp.wait_ge(d_perm, i + 1)
                sp.dma_start(k.dst_rows[i * CG:(i + 1) * CG, :],
                             perm[0][i][:, :, :].rearrange("g t p -> g (t p)")).then_inc(rows_out, 16)
                sp.wait_ge(s_perm, i + 1)
                sp.dma_start(k.src_rows[i * CG:(i + 1) * CG, :],
                             perm[1][i][:, :, :].rearrange("g t p -> g (t p)")).then_inc(rows_out, 16)
            sp.wait_ge(rows_out, 32 * CH)

        def landed(i):
            n = min(S.FULL, (i + 1) * CG) - i * CG
            return 32 * (1 + CG - n)

        @block.gpsimd
        def _(pool):
            pool.memset(k.ident[:, :], 0.0).then_inc(cst0, 1)
            pool.memset(k.identb[:, :], 0.0).then_inc(cst0, 1)
            pool.memset(k.ones[:, :], 1.0).then_inc(cst0, 1)
            pool.memset(k.valid[:, :], 1.0).then_inc(cst0, 1)
            pool.memset(k.zeros[:, :], 0.0).then_inc(cst0, 1)
            pool.wait_ge(cst0, 5)
            for m in (k.ident, k.identb):
                pool.affine_select(out=m[:, :], in_=m[:, :], compare_op=ALU.not_equal, fill=1.0, base=0,
                                   pattern=[[-1, P]], channel_multiplier=1).then_inc(cst, 1)
            pool.affine_select(out=k.valid[:, :], in_=k.valid[:, :], compare_op=ALU.is_ge, fill=0.0,
                               base=S.N - 1, pattern=[[-P, S.BP]], channel_multiplier=-1).then_inc(cst, 1)
            pool.iota(iota_i[:, :], pattern=[[1, W * P]], base=0, channel_multiplier=0).then_inc(cst, 1)
            pool.iota(pidx_i[:, :], pattern=[[0, 1]], base=0, channel_multiplier=1).then_inc(cst, 1)
            pool.iota(k.weight[:, :].bitcast(i32), pattern=[[0, 1]], base=(187 << 23),
                      channel_multiplier=-(1 << 23)).then_inc(cst, 1)
            pool.wait_ge(reduced, CH)
            last = flt[0][CH - 1]
            pool.affine_select(out=last[:, :], in_=last[:, :], compare_op=ALU.is_ge, fill=-1.0,
                               base=GE * (S.FULL - (CH - 1) * CG) - S.DUP, pattern=[[1, GE]],
                               channel_multiplier=-GE).then_inc(masked, 1)

        @block.vector
        def _(v):
            link = chain(v, dve)
            v.wait_ge(cst, 6)
            v.tensor_copy(k.iota[:, :], iota_i[:, :])
            link(v.tensor_copy(k.pidx[:, :], pidx_i[:, :]))
            v.tensor_scalar_add(k.trash[:, :], k.pidx[:, :], float(S.N))
            v.tensor_scalar_mul(k.weight25[:, :], k.weight[:, :], 2.5)
            for i in range(CH):
                v.wait_ge(idx_in[i], landed(i))
                link(v.tensor_copy(flt[0][i][:, :], raw[0][i][:, :]))
                v.tensor_reduce(lohi[:, i, 0:1], flt[0][i][:, :], X, ALU.min)
                link(v.tensor_reduce(lohi[:, i, 1:2], flt[0][i][:, :], X, ALU.max))
                v.sem_inc(reduced, 1)
                link(v.tensor_copy(lohi_i[:, i, :], lohi[:, i, :]))
                link(v.tensor_scalar(lohi_i[:, i, :], lohi_i[:, i, :], 7, None, ALU.arith_shift_right))
                link(v.tensor_copy(blk[:, i, :], lohi_i[:, i, :]))
                link(v.tensor_tensor(blk[:, i, 1:2], blk[:, i, 1:2], blk[:, i, 0:1], ALU.subtract))
                v.tensor_scalar(qrep[:, i, 0, :], k.ones[0:CG, :], blk[:, i, 0:1], None, ALU.mult)
                v.tensor_scalar(qrep[:, i, 1, :], k.ones[0:CG, :], blk[:, i, 1:2], None,
                                ALU.mult).then_inc(q_ready, 1)
                if i == CH - 1:
                    v.wait_ge(masked, 1)
                v.sem_inc(d_flt, 1)
                v.tensor_copy(perm[0][i][:, :, :],
                              flt[0][i][:, :].rearrange("g (p t) -> g t p", t=T)).then_inc(d_perm, 1)
                v.wait_ge(tr_d, i + 1)
                g0 = i * CG
                for h in range(2):
                    v.tensor_copy(k.dst[:, g0:g0 + CG, 4 * h:4 * h + 4],
                                  ps_d[h][:, :, 0:CG].rearrange("p t g -> p g t"))
                v.tensor_copy(k.first[:, g0:g0 + CG], ps_q[:, 0, 0:CG])
                v.tensor_copy(span[:, g0:g0 + CG], ps_q[:, 1, 0:CG]).then_inc(ev_d, 1)
            v.wait_ge(ev_d, CH)
            link(v.tensor_reduce(smax[:, 0:1], span[:, :], X, ALU.max))
            link(v.tensor_copy(smax_i[:, 0:1], smax[:, 0:1]))
            link(v.tensor_scalar(smax_i[:, 1:2], smax_i[:, 0:1], 1, None, ALU.arith_shift_right))
            link(v.tensor_copy(smax[:, 1:2], smax_i[:, 1:2]))
            link(v.tensor_scalar_add(smax[:, 1:2], smax[:, 1:2], 1.0))
            link(v.tensor_copy(k.passes[:, :], smax[:, 1:2]))

        @block.scalar
        def _(a):
            for i in range(CH):
                a.wait_ge(idx_in[i], landed(i))
                a.activation(flt[1][i][:, :], raw[1][i][:, :], ACT.Copy).then_inc(s_flt, 1)
                a.wait_ge(s_flt, i + 1)
                a.activation(perm[1][i][:, :, :], flt[1][i][:, :].rearrange("g (p t) -> g t p", t=T),
                             ACT.Copy).then_inc(s_perm, 1)
                a.wait_ge(tr_s, i + 1)
                g0 = i * CG
                for h in range(2):
                    last = a.activation(k.src[:, g0:g0 + CG, 4 * h:4 * h + 4],
                                        ps_s[h][:, :, 0:CG].rearrange("p t g -> p g t"), ACT.Copy)
                last.then_inc(ev_s, 1)

        @block.tensor
        def _(pe):
            pe.wait_ge(cst, 6)
            for i in range(CH):
                ident = k.ident[0:CG, 0:CG]
                pe.wait_ge(q_ready, i + 1)
                pe.wait_ge(d_flt, i + 1)
                need(pe, ev_d, i)
                for w in range(2):
                    pe.matmul(ps_q[:, w, 0:CG], qrep[:, i, w, :], ident, start=True, stop=True)
                for t in range(T):
                    last = pe.transpose(ps_d[t // 4][:, t % 4, 0:CG], flt[0][i][:, t::T], ident)
                last.then_inc(tr_d, 1)
                pe.wait_ge(s_flt, i + 1)
                need(pe, ev_s, i)
                for t in range(T):
                    last = pe.transpose(ps_s[t // 4][:, t % 4, 0:CG], flt[1][i][:, t::T], ident)
                last.then_inc(tr_s, 1)


def setup_nodes(nc, S, k, sem, x, W1, b1, W2, b2, root, bias, gamma, beta, Wmsg_lin, Wupd_lin):
    with ExitStack() as c:
        def sb(name, shape, dt):
            return c.enter_context(nc.sbuf_tensor(name, shape, dt))
        w1 = sb("w1raw", [D, 256], f32)
        r1, r2 = sb("w1r1", [D, 256], f32), sb("w1r2", [D, 256], f32)
        part = [sb(f"w1part{i}", [D, 256], bf16) for i in range(3)]
        cleared, w_in, packed, dve, zeroed = (sem(n) for n in
                                              ("cleared", "w_in", "packed", "sn_dve", "zeroed"))
        split = sem("w1split")
        block = c.enter_context(nc.Block())

        @block.gpsimd
        def _(pool):
            pool.memset(k.x[:, S.B - 1:, :], 0.0).then_inc(cleared, 1)
            for t in (k.bd_pre, k.bd_lin, k.bd_out):
                pool.memset(t[:, :, :], 0.0).then_inc(cleared, 1)

        @block.sync
        def _(sp):
            sp.dma_start(w1[:, :], W1).then_inc(w_in, 16)
            for j in range(2):
                sp.dma_start(k.b1[:, j:j + 1],
                             b1[j * P:(j + 1) * P].rearrange("(p a) -> p a", a=1)).then_inc(packed, 16)
            sp.dma_start(k.W2[:, :, :], W2.rearrange("(j p) n -> p j n", p=P)).then_inc(packed, 16)
            for t, w in ((k.bias, bias), (k.gamma, gamma), (k.beta, beta)):
                sp.dma_start(t[:, :], w.partition_broadcast(P)).then_inc(packed, 16)
            sp.wait_ge(cleared, 4)
            sp.dma_start(k.x[:, 0:S.B - 1, :],
                         x[0:P * (S.B - 1), :].rearrange("(c p) f -> p c f", p=P)).then_inc(packed, 16)
            sp.dma_start(k.x[0:S.REST, S.B - 1, :], x[P * (S.B - 1):, :]).then_inc(packed, 16)
            b2m = b2.rearrange("(i o) -> i o", o=D)
            for b in range(T):
                rows = slice(D * b, D * (b + 1))
                sp.dma_start(k.bd_pre[rows, b, 0:D], b2m).then_inc(packed, 16)
                sp.dma_start(k.bd_pre[rows, b, D:2 * D], root).then_inc(packed, 16)
                sp.dma_start(k.bd_lin[rows, b, :], Wmsg_lin).then_inc(packed, 16)
                sp.dma_start(k.bd_out[rows, b, :], Wupd_lin).then_inc(packed, 16)
            sp.wait_ge(split, 1)
            for r, n in enumerate((0, 1, 2, 0, 1, 0)):
                sp.dma_start(k.W1p[D * r:D * (r + 1), :], part[n][:, :]).then_inc(packed, 16)
            sp.wait_ge(packed, 16 * (6 + 2 + 4 * T + 6))

        @block.scalar
        def _(a):
            n = S.N * D // 125
            per = [(s, min(512, n - s)) for s in range(0, n, 512)]
            for t in range(T):
                flat = k.sums[t][0:S.N, :].rearrange("a b -> (a b)").rearrange("(p f) -> p f", p=125)
                for s, m in per:
                    a.dma_start(flat[:, s:s + m], k.zeros[0:125, 0:m]).then_inc(zeroed, 16)
                a.dma_start(k.sums[t][S.N:, :], k.zeros[:, 0:D]).then_inc(zeroed, 16)
            a.wait_ge(zeroed, 16 * T * (len(per) + 1))

        @block.vector
        def _(v):
            link = chain(v, dve)
            v.wait_ge(w_in, 16)
            link(v.tensor_copy(part[0][:, :], w1[:, :]))
            link(v.tensor_tensor(r1[:, :], w1[:, :], part[0][:, :], ALU.subtract))
            link(v.tensor_copy(part[1][:, :], r1[:, :]))
            link(v.tensor_tensor(r2[:, :], r1[:, :], part[1][:, :], ALU.subtract))
            v.tensor_copy(part[2][:, :], r2[:, :]).then_inc(split, 1)


class Norm:

    def __init__(self, nc, S, sem, c, name):
        def sb(n, shape):
            return c.enter_context(nc.sbuf_tensor(f"{name}_{n}", shape, f32))
        self.sq = sb("sq", [P, S.BP, D])
        self.mean, self.var, self.sd = sb("mean", [P, S.BP]), sb("var", [P, S.BP]), sb("sd", [P, S.BP])
        self.shape = [P, S.BP, D]
        self.var_ready, self.sd_ready = sem(f"{name}_var"), sem(f"{name}_sd")

    def vector(self, v, link, x, h):
        def over(t):
            return t[:, :].unsqueeze(2).broadcast_to(self.shape)
        link(v.tensor_reduce(self.mean[:, :], x[:, :, :], X, ALU.add))
        link(v.tensor_scalar_mul(self.mean[:, :], self.mean[:, :], 1.0 / D))
        link(v.tensor_tensor(h[:, :, :], x[:, :, :], over(self.mean), ALU.subtract))
        link(v.tensor_tensor(self.sq[:, :, :], h[:, :, :], h[:, :, :], ALU.mult))
        link(v.tensor_reduce(self.var[:, :], self.sq[:, :, :], X, ALU.add))
        v.tensor_scalar(self.var[:, :], self.var[:, :], 1.0 / D, LN_EPS,
                        ALU.mult, ALU.add).then_inc(self.var_ready, 1)
        v.wait_ge(self.sd_ready, 1)
        link(v.reciprocal(self.sd[:, :], self.sd[:, :]))
        link(v.tensor_tensor(h[:, :, :], h[:, :, :], over(self.sd), ALU.mult))
        link(v.tensor_scalar_max(h[:, :, :], h[:, :, :], 0.0))

    def scalar(self, a):
        a.wait_ge(self.var_ready, 1)
        a.activation(self.sd[:, :], self.var[:, :], ACT.Sqrt).then_inc(self.sd_ready, 1)


class NodeLinear:

    def __init__(self, nc, S, sem, c, name, src, weights, width):
        self.S, self.k_src, self.weights, self.width = S, src, weights, width
        self.pieces = max(1, T * width // 512)
        self.cols = T * width // self.pieces
        self.xT = [c.enter_context(nc.sbuf_tensor(f"{name}_xT{i}", [P, P], f32)) for i in range(2)]
        self.ps_t = [c.enter_context(nc.psum_tensor(f"{name}_pt{i}", [P, P], f32)) for i in range(2)]
        self.ring = max(2, self.pieces)
        self.out = [c.enter_context(nc.psum_tensor(f"{name}_po{i}", [P, self.cols], f32))
                    for i in range(self.ring)]
        self.turned, self.copied = sem(f"{name}_turned"), sem(f"{name}_copied")
        self.done, self.taken = sem(f"{name}_done"), sem(f"{name}_taken")

    def bank(self, s, j):
        return self.out[s if self.pieces == 1 else j]

    def tensor(self, pe, ident):
        def body(c, s, use):
            need(pe, self.copied, c - 1)
            pe.transpose(self.ps_t[s][:, :],
                         self.k_src[:, c * T:(c + 1) * T, :].rearrange("p b f -> p (b f)"),
                         ident).then_inc(self.turned, 1)
            pe.wait_ge(self.copied, c + 1)
            w = self.weights[:, :, :].rearrange("p b w -> p (b w)")
            for j in range(self.pieces):
                need(pe, self.taken, c * self.pieces + j + 1 - self.ring)
                pe.matmul(self.bank(s, j)[:, :], self.xT[s][:, :], w[:, j * self.cols:(j + 1) * self.cols],
                          start=True, stop=True).then_inc(self.done, 1)
        for c in range(self.S.NC):
            body(c, c % 2, c // 2)

    def scalar(self, a, extra=None):
        def body(c, s, use):
            a.wait_ge(self.turned, c + 1)
            need(a, self.done, (c - 1) * self.pieces)
            a.activation(self.xT[s][:, :], self.ps_t[s][:, :], ACT.Copy).then_inc(self.copied, 1)
            if extra is not None:
                extra(c, s)
        each(a, self.S.NC, body, head=2 + self.S.NC % 2)


def pre_layer(nc, S, k, sem, c):
    rows = c.enter_context(nc.sbuf_tensor("rows", [P, S.BP, 2 * D], f32))
    norm = Norm(nc, S, sem, c, "ln0")
    lin = NodeLinear(nc, S, sem, c, "pre", k.h, k.bd_pre, 2 * D)
    h_ready, rows_ready, stored = sem("h0_ready"), sem("rows_ready"), sem("rows_stored")
    dve = sem("pre_dve")
    block = c.enter_context(nc.Block())

    @block.vector
    def _(v):
        link = chain(v, dve)
        norm.vector(v, link, k.x, k.h)
        v.sem_inc(h_ready, 1)
        v.tensor_copy(rows[:, :, 0:D], k.h[:, :, :])

        def body(ch, s, use):
            v.wait_ge(lin.done, ch + 1)
            y = lin.bank(s, 0)[:, :].rearrange("p (b w) -> p b w", w=2 * D)
            v.tensor_copy(rows[:, bass.ds(ch * T, T), D:2 * D], y[:, :, 0:D])
            v.tensor_tensor(k.agg[:, bass.ds(ch * T, T), :], y[:, :, D:2 * D],
                            k.bias[:, :].unsqueeze(1).broadcast_to([P, T, D]), ALU.add
                            ).then_inc(lin.taken, 1)
        each(v, S.NC, body, head=2 + S.NC % 2)
        v.wait_ge(lin.taken, S.NC)
        v.sem_inc(rows_ready, 1)

    @block.scalar
    def _(a):
        norm.scalar(a)
        lin.scalar(a)

    @block.tensor
    def _(pe):
        pe.wait_ge(h_ready, 1)
        lin.tensor(pe, k.ident[:, :])

    @block.sync
    def _(sp):
        sp.wait_ge(rows_ready, 1)
        sp.dma_start(k.rows[0:P * (S.B - 1), :].rearrange("(c p) f -> p c f", p=P),
                     rows[:, 0:S.B - 1, :]).then_inc(stored, 16)
        sp.dma_start(k.rows[P * (S.B - 1):, :], rows[0:S.REST, S.B - 1, :]).then_inc(stored, 16)
        sp.wait_ge(stored, 32)


def first_windows(nc, S, k, sem, c, name):
    block = c.enter_context(nc.Block())
    done = sem(f"{name}_first")

    @block.vector
    def _(v):
        v.tensor_copy(k.base[:, :], k.first[:, :]).then_inc(done, 1)
        v.wait_ge(done, 1)


def set_windows(v, link, S, k):
    link(v.tensor_scalar_min(k.win[:, :], k.base[:, :], float(S.B)))
    v.tensor_copy(k.win_i[:, :], k.win[0:1, :])
    link(v.tensor_scalar_add(k.base[:, :], k.base[:, :], float(W)))


def layer0(nc, S, k, sem, c, ea16, n_passes):
    G = S.G

    def sb(name, shape, dt):
        return c.enter_context(nc.sbuf_tensor(name, shape, dt))

    def ps(name, shape, dt=f32):
        return c.enter_context(nc.psum_tensor(name, shape, dt))

    ea = [sb(f"ea{s}", [P, T, D], f32) for s in range(2)]
    ea_parts = sb("ea_parts", [P, T, 6, D], bf16)
    ea_res = sb("ea_res", [P, T, D], f32)
    eT = [sb(f"eT{s}", [96, GE], bf16) for s in range(2)]
    hT = [sb(f"hT{s}", [P, 2, 512], f32) for s in range(2)]
    idx = [sb(f"idx{s}", [P, T], i32) for s in range(2)]
    xg = [sb(f"xg{s}", [P, T, 2 * D], f32) for s in range(2)]
    prod = [sb(f"prod{s}", [P, 2, D, D], f32) for s in range(2)]
    msg = [sb(f"msg{s}", [P, T, D], f32) for s in range(2)]
    msg_res = sb("msg_res", [P, T, D], f32)
    parts = [sb(f"parts{s}", [P, T, 3, D], bf16) for s in range(2)]
    hot = [sb(f"hot{s}", [P, T, W * P], bf16) for s in range(2)]
    win_sum = sb("win_sum", [P, W, D], f32)
    ps_e = ps("ps_e", [96, GE], bf16)
    ps_h = [ps(f"ps_h{j}", [P, 512]) for j in range(2)]
    ps_w = [ps(f"ps_w{u}", [P, 2, D, D]) for u in range(4)]
    ps_a = ps("ps_a", [P, W, 3, D])

    names = ("l0_dve ea_used e_hi e_res e_mid e_lo e_turned eT_ready hmm relued wmm multiplied "
             "reduced0 idx_ready msg_ready m_hi m_res m_mid m_lo hot_ready scattered ps_a_free added "
             "tables0 gathers_begun").split()
    q = {n: sem(n) for n in names}
    ea_in = [sem(f"ea_in{s}") for s in range(2)]
    xg_in = [[sem(f"xg_in{s}{t}") for t in range(T)] for s in range(2)]
    first_windows(nc, S, k, sem, c_ := ExitStack(), "l0")
    c_.close()

    with nc.Fori(0, n_passes) as _:
        with nc.Block() as block:

            @block.sync
            def _(sp):
                def load(g, s, use):
                    e0 = min(g * GE, S.E - GE) if isinstance(g, int) else sp.snap(g * GE)
                    need(sp, q["ea_used"], g - 1)
                    sp.dma_start(ea[s][:, :, :].rearrange("p t f -> p (t f)"),
                                 ea16[bass.ds(e0, GE), :].rearrange("(p t) f -> p (t f)", t=T)
                                 ).then_inc(ea_in[s], 16)
                each(sp, G, load, tail=2)

            @block.gpsimd
            def _(pool):
                def gather(g, s, use):
                    pool.wait_ge(q["idx_ready"], g + 1)
                    need(pool, q["msg_ready"], g - 1)
                    pool.sem_inc(q["gathers_begun"], 1)
                    for t in range(T):
                        pool.indirect_dma_start(
                            xg[s][:, t, :], None, k.rows,
                            bass.IndirectOffsetOnAxis(ap=idx[s][:, t:t + 1], axis=0)
                        ).then_inc(xg_in[s][t], 16)
                each(pool, G, gather)
                pool.wait_ge(q["msg_ready"], G)
                pool.dma_reset()

            @block.scalar
            def _(a):
                def indices(g, s):
                    need(a, q["multiplied"], 4 * (g - 1))
                    a.activation(idx[s][:, :], k.src[:, bass.ds(g, 1), :].rearrange("p g t -> p (g t)"),
                                 ACT.Copy).then_inc(q["idx_ready"], 1)

                def edges_hi(g, s, use):
                    a.wait_ge(ea_in[s], 16 * (use + 1))
                    need(a, q["e_turned"], g)
                    a.activation(ea_parts[:, :, 0:3, :],
                                 ea[s][:, :, :].unsqueeze(2).broadcast_to([P, T, 3, D]),
                                 ACT.Copy).then_inc(q["e_hi"], 1)

                def edges_mid(g):
                    a.wait_ge(q["e_res"], g + 1)
                    a.activation(ea_parts[:, :, 3:5, :],
                                 ea_res[:, :, :].unsqueeze(2).broadcast_to([P, T, 2, D]),
                                 ACT.Copy).then_inc(q["e_mid"], 1)

                def edges_T(g, s):
                    a.wait_ge(q["e_turned"], g + 1)
                    need(a, q["hmm"], 4 * (g - 1))
                    a.activation(eT[s][:, :], ps_e[:, :], ACT.Copy).then_inc(q["eT_ready"], 1)

                def relu(c, s):
                    need(a, q["wmm"], 2 * (c - 1))
                    for j in range(2):
                        a.wait_ge(q["hmm"], 2 * c + j + 1)
                        a.activation(hT[s][:, j, :], ps_h[j][:, :], ACT.Relu,
                                     bias=k.b1[:, j:j + 1]).then_inc(q["relued"], 1)

                def msg_hi(g, s):
                    a.wait_ge(q["msg_ready"], g + 1)
                    need(a, q["scattered"], g - 1)
                    a.activation(parts[s][:, :, 0, :], msg[s][:, :, :], ACT.Copy).then_inc(q["m_hi"], 1)

                def msg_mid(g, s):
                    a.wait_ge(q["m_res"], g + 1)
                    a.activation(parts[s][:, :, 1, :], msg_res[:, :, :], ACT.Copy).then_inc(q["m_mid"], 1)

                indices(0, 0)
                edges_hi(0, 0, 0)
                edges_mid(0)
                edges_T(0, 0)
                relu(0, 0)
                edges_hi(1, 1, 0)
                edges_mid(1)

                def body(g, s, use):
                    ahead = not isinstance(g, int)
                    relu(g * 2 + 1, 1)
                    if ahead or g + 1 < G:
                        indices(g + 1, 1 - s)
                    if ahead or g >= 1:
                        msg_hi(g - 1, 1 - s)
                        msg_mid(g - 1, 1 - s)
                    if ahead or g + 1 < G:
                        edges_T(g + 1, 1 - s)
                    if ahead or g + 2 < G:
                        edges_hi(g + 2, s, use + 1)
                    if ahead or g + 1 < G:
                        relu(g * 2 + 2, 0)
                    if ahead or g + 2 < G:
                        edges_mid(g + 2)
                each(a, G, body, head=4, tail=2)
                msg_hi(G - 1, 1)
                msg_mid(G - 1, 1)

            @block.tensor
            def _(pe):
                def turn(g):
                    pe.wait_ge(q["e_lo"], g + 1)
                    need(pe, q["eT_ready"], g)
                    for t in range(T):
                        last = pe.transpose(ps_e[:, t * P:(t + 1) * P],
                                            ea_parts[:, t, :, :].rearrange("p a f -> p (a f)"),
                                            k.identb[:, :])
                    last.then_inc(q["e_turned"], 1)

                def hidden(c, g, half, s):
                    if half == 0:
                        pe.wait_ge(q["eT_ready"], g + 1)
                    for j in range(2):
                        need(pe, q["relued"], 2 * (c - 1) + j + 1)
                        pe.matmul(ps_h[j][:, :], k.W1p[:, j * P:(j + 1) * P],
                                  eT[s][:, half * 512:(half + 1) * 512],
                                  start=True, stop=True).then_inc(q["hmm"], 1)

                def edge_weights(c, half, units):
                    pe.wait_ge(q["relued"], 2 * c + 2)
                    for u in units:
                        need(pe, q["multiplied"], 2 * c + u - 3)
                        bank = ps_w[2 * half + u]
                        for w in range(2):
                            col = (2 * u + w) * P
                            for j in range(2):
                                last = pe.matmul(bank[:, w, :, :].rearrange("p i o -> p (i o)"),
                                                 hT[half][:, j, col:col + P], k.W2[:, j, :],
                                                 start=(j == 0), stop=(j == 1))
                        last.then_inc(q["wmm"], 1)

                def scatter(g, s):
                    pe.wait_ge(q["m_lo"], g + 1)
                    pe.wait_ge(q["hot_ready"], g + 1)
                    need(pe, q["ps_a_free"], g)
                    for t in range(T):
                        for b in range(W):
                            last = pe.matmul(ps_a[:, b, :, :].rearrange("p a o -> p (a o)"),
                                             hot[s][:, t, b * P:(b + 1) * P],
                                             parts[s][:, t, :, :].rearrange("p a o -> p (a o)"),
                                             start=(t == 0 and b == 0), stop=(t == T - 1),
                                             skip_group_check=True)
                    last.then_inc(q["scattered"], 1)

                turn(0)
                hidden(0, 0, 0, 0)

                def body(g, s, use):
                    more = not isinstance(g, int) or g + 1 < G
                    hidden(g * 2 + 1, g, 1, s)
                    edge_weights(g * 2, 0, (0, 1))
                    if more:
                        turn(g + 1)
                    edge_weights(g * 2 + 1, 1, (0,))
                    if more:
                        hidden(g * 2 + 2, g + 1, 0, 1 - s)
                    edge_weights(g * 2 + 1, 1, (1,))
                    if not isinstance(g, int) or g >= 1:
                        scatter(g - 1, 1 - s)
                each(pe, G, body, head=4, tail=2)
                scatter(G - 1, 1)

            @block.vector
            def _(v):
                link = chain(v, q["l0_dve"])
                set_windows(v, link, S, k)
                link(v.scalar_tensor_tensor(k.rel[:, :, :],
                                            k.win[:, :].unsqueeze(2).broadcast_to([P, G, T]), float(-P),
                                            k.dst[:, :, :], ALU.mult, ALU.add))

                def edges_res(g, s):
                    v.wait_ge(q["e_hi"], g + 1)
                    need(v, q["e_lo"], g)
                    v.tensor_tensor(ea_res[:, :, :], ea[s][:, :, :], ea_parts[:, :, 0, :],
                                    ALU.subtract).then_inc(q["e_res"], 1)
                    v.wait_ge(q["e_res"], g + 1)
                    v.sem_inc(q["ea_used"], 1)

                def edges_lo(g):
                    v.wait_ge(q["e_mid"], g + 1)
                    v.tensor_tensor(ea_parts[:, :, 5, :], ea_res[:, :, :], ea_parts[:, :, 3, :],
                                    ALU.subtract).then_inc(q["e_lo"], 1)

                def unit(g, s, u, use):
                    n = g * 4 + u
                    v.wait_ge(q["wmm"], n + 1)
                    for t in (2 * u, 2 * u + 1):
                        v.wait_ge(xg_in[s][t], 16 * (use + 1))
                    need(v, q["reduced0"], n - 1)
                    v.tensor_tensor(prod[u % 2][:, :, :, :], ps_w[u][:, :, :, :],
                                    xg[s][:, 2 * u:2 * u + 2, 0:D].unsqueeze(3).broadcast_to([P, 2, D, D]),
                                    ALU.mult).then_inc(q["multiplied"], 1)

                def sum_unit(g, s, u):
                    n = g * 4 + u
                    v.wait_ge(q["multiplied"], n + 1)
                    v.tensor_reduce(msg[s][:, 2 * u:2 * u + 2, :],
                                    prod[u % 2][:, :, :, :].rearrange("p t i o -> p t o i"), X,
                                    ALU.add).then_inc(q["reduced0"], 1)

                def add_bias(g, s):
                    v.wait_ge(q["reduced0"], g * 4 + 4)
                    v.tensor_tensor(msg[s][:, :, :], msg[s][:, :, :], xg[s][:, :, D:2 * D],
                                    ALU.add).then_inc(q["msg_ready"], 1)

                def msg_residue(g, s):
                    v.wait_ge(q["m_hi"], g + 1)
                    need(v, q["m_lo"], g)
                    v.tensor_tensor(msg_res[:, :, :], msg[s][:, :, :], parts[s][:, :, 0, :],
                                    ALU.subtract).then_inc(q["m_res"], 1)

                def msg_lo(g, s):
                    v.wait_ge(q["m_mid"], g + 1)
                    v.tensor_tensor(parts[s][:, :, 2, :], msg_res[:, :, :], parts[s][:, :, 1, :],
                                    ALU.subtract).then_inc(q["m_lo"], 1)

                def one_hot(g, s, tiles):
                    if tiles[0] == 0:
                        need(v, q["scattered"], g - 1)
                    for t in tiles:
                        last = v.tensor_scalar(hot[s][:, t, :], k.iota[:, :],
                                               k.rel[:, bass.ds(g, 1), t:t + 1].rearrange("p g t -> p (g t)"),
                                               None, ALU.is_equal)
                    if tiles[-1] == T - 1:
                        last.then_inc(q["hot_ready"], 1)

                def add_window(g):
                    v.wait_ge(q["scattered"], g + 1)
                    need(v, q["added"], g)
                    v.tensor_reduce(win_sum[:, :, :], ps_a[:, :, :, :].rearrange("p w a o -> p w o a"), X,
                                    ALU.add).then_inc(q["ps_a_free"], 1)
                    at = v.value_load(k.win_i[0:1, bass.ds(g, 1)], min_val=0, max_val=S.B)
                    v.wait_ge(q["ps_a_free"], g + 1)
                    v.tensor_tensor(k.agg[:, bass.ds(at, W), :], k.agg[:, bass.ds(at, W), :],
                                    win_sum[:, :, :], ALU.add).then_inc(q["added"], 1)

                edges_res(0, 0)
                edges_lo(0)
                edges_res(1, 1)
                edges_lo(1)

                def body(g, s, use):
                    ahead = not isinstance(g, int)
                    unit(g, s, 0, use)
                    if ahead or g >= 1:
                        msg_residue(g - 1, 1 - s)
                    sum_unit(g, s, 0)
                    if ahead or g >= 2:
                        add_window(g - 2)
                    unit(g, s, 1, use)
                    one_hot(g, s, (0, 1, 2, 3))
                    sum_unit(g, s, 1)
                    if ahead or g >= 1:
                        msg_lo(g - 1, 1 - s)
                    unit(g, s, 2, use)
                    one_hot(g, s, (4, 5, 6, 7))
                    sum_unit(g, s, 2)
                    unit(g, s, 3, use)
                    if ahead or g + 2 < G:
                        edges_res(g + 2, s)
                    sum_unit(g, s, 3)
                    add_bias(g, s)
                    if ahead or g + 2 < G:
                        edges_lo(g + 2)
                each(v, G, body, head=4, tail=2)
                msg_residue(G - 1, 1)
                msg_lo(G - 1, 1)
                add_window(G - 2)
                add_window(G - 1)
                v.wait_ge(q["added"], G)

        clear_all(nc, [*q.values(), *ea_in, *(x for r in xg_in for x in r)])


def between(nc, S, k, sem, c, Wmsg):
    def sb(name, shape, dt=f32):
        return c.enter_context(nc.sbuf_tensor(name, shape, dt))
    bd_msg = sb("bd_msg", [P, T, P])
    t0, sums, mean, var = sb("bn_t0", [P, S.BP, D]), sb("bn_s", [P, D]), sb("bn_m", [P, D]), sb("bn_v", [P, D])
    res = [sb(f"q_res{i}", [P, 4, P]) for i in range(2)]
    ps_m = c.enter_context(nc.psum_tensor("ps_m", [P, 2, D], f32))
    norm = Norm(nc, S, sem, c, "ln1")
    lin = NodeLinear(nc, S, sem, c, "msg", k.h, bd_msg, P)
    n = {x: sem(x) for x in ("bt_dve bd_clear bd_in bn_part bn_sum bn_var bn_sd h1_ready "
                             "q_hi q_res q_mid q_lo").split()}
    block = c.enter_context(nc.Block())

    @block.gpsimd
    def _(pool):
        pool.memset(bd_msg[:, :, :], 0.0).then_inc(n["bd_clear"], 1)

    @block.sync
    def _(sp):
        sp.wait_ge(n["bd_clear"], 1)
        for b in range(T):
            sp.dma_start(bd_msg[D * b:D * (b + 1), b, :],
                         Wmsg.rearrange("i j h -> i (j h)")).then_inc(n["bd_in"], 16)

    @block.vector
    def _(v):
        link = chain(v, n["bt_dve"])
        valid = k.valid[:, :].unsqueeze(2).broadcast_to([P, S.BP, D])

        def over(t):
            return t[:, :].unsqueeze(1).broadcast_to([P, S.BP, D])
        agg = k.agg[:, :, :]
        link(v.tensor_tensor(t0[:, :, :], agg, valid, ALU.mult))
        v.tensor_reduce(sums[:, :], t0[:, :, :].rearrange("p b f -> p f b"), X, ALU.add).then_inc(n["bn_part"], 1)
        v.wait_ge(n["bn_sum"], 1)
        link(v.tensor_scalar_mul(mean[:, :], ps_m[:, 0, :], 1.0 / S.N))
        link(v.tensor_tensor(agg, agg, over(mean), ALU.subtract))
        link(v.tensor_tensor(agg, agg, valid, ALU.mult))
        link(v.tensor_tensor(t0[:, :, :], agg, agg, ALU.mult))
        v.tensor_reduce(sums[:, :], t0[:, :, :].rearrange("p b f -> p f b"), X, ALU.add).then_inc(n["bn_part"], 1)
        v.wait_ge(n["bn_sum"], 2)
        v.tensor_scalar(var[:, :], ps_m[:, 1, :], 1.0 / S.N, BN_EPS, ALU.mult, ALU.add).then_inc(n["bn_var"], 1)
        v.wait_ge(n["bn_sd"], 1)
        link(v.reciprocal(var[:, :], mean[:, :]))
        link(v.tensor_tensor(var[:, :], var[:, :], k.gamma[:, :], ALU.mult))
        link(v.tensor_tensor(agg, agg, over(var), ALU.mult))
        link(v.tensor_tensor(agg, agg, over(k.beta), ALU.add))
        link(v.tensor_scalar_max(agg, agg, 0.0))
        link(v.tensor_tensor(k.x[:, :, :], k.x[:, :, :], agg, ALU.add))
        norm.vector(v, link, k.x, k.h)
        v.sem_inc(n["h1_ready"], 1)
        link(v.tensor_tensor(k.x[:, :, :], k.x[:, :, :], k.h[:, :, :], ALU.add))

        def body(c_, s, use):
            for j in range(2):
                piece = c_ * 2 + j
                v.wait_ge(n["q_hi"], piece + 1)
                need(v, n["q_lo"], piece - 1)
                b0 = c_ * T + 4 * j
                y = lin.bank(s, j)[:, :].rearrange("p (b w) -> p b w", w=P)
                v.tensor_tensor(res[j][:, :, :], y, k.Q[:, bass.ds(b0, 4), 0, :],
                                ALU.subtract).then_inc(n["q_res"], 1)
                v.wait_ge(n["q_res"], piece + 1)
                v.sem_inc(lin.taken, 1)
                v.wait_ge(n["q_mid"], piece + 1)
                v.tensor_tensor(k.Q[:, bass.ds(b0, 4), 2, :], res[j][:, :, :],
                                k.Q[:, bass.ds(b0, 4), 1, :], ALU.subtract).then_inc(n["q_lo"], 1)
        each(v, S.NC, body, head=2 + S.NC % 2)

    @block.scalar
    def _(a):
        a.wait_ge(n["bn_var"], 1)
        a.activation(mean[:, :], var[:, :], ACT.Sqrt).then_inc(n["bn_sd"], 1)
        norm.scalar(a)

        def parts(c_, s, use):
            a.wait_ge(lin.turned, c_ + 1)
            need(a, lin.done, (c_ - 1) * 2)
            a.activation(lin.xT[s][:, :], lin.ps_t[s][:, :], ACT.Copy).then_inc(lin.copied, 1)
            for j in range(2):
                piece = c_ * 2 + j
                b0 = c_ * T + 4 * j
                a.wait_ge(lin.done, piece + 1)
                y = lin.bank(s, j)[:, :].rearrange("p (b w) -> p b w", w=P)
                a.activation(k.Q[:, bass.ds(b0, 4), 0, :], y, ACT.Copy).then_inc(n["q_hi"], 1)
                a.wait_ge(n["q_res"], piece + 1)
                a.activation(k.Q[:, bass.ds(b0, 4), 1, :], res[j][:, :, :], ACT.Copy).then_inc(n["q_mid"], 1)
        each(a, S.NC, parts, head=2 + S.NC % 2)

    @block.tensor
    def _(pe):
        for r in range(2):
            pe.wait_ge(n["bn_part"], r + 1)
            pe.matmul(ps_m[:, r, :], k.ones[:, :], sums[:, :], start=True, stop=True).then_inc(n["bn_sum"], 1)
        pe.wait_ge(n["bd_in"], 16 * T)
        pe.wait_ge(n["h1_ready"], 1)
        lin.tensor(pe, k.ident[:, :])


def layer1(nc, S, k, sem, c, ea8, n_passes):
    G, J = S.G, ea8.shape[1]
    NORM = float(1.0 / np.float32(np.sqrt(D * J)))

    def sb(name, shape, dt):
        return c.enter_context(nc.sbuf_tensor(name, shape, dt))

    def ps(name, shape, dt=f32):
        return c.enter_context(nc.psum_tensor(name, shape, dt))

    ea = [sb(f"e8_{s}", [P, T, J], f32) for s in range(2)]
    dst_row = [sb(f"dst_row{s}", [P, GE], i16) for s in range(2)]
    src_row = [sb(f"src_row{s}", [P, T, P], i16) for s in range(2)]
    hotT = [sb(f"hotT{s}", [P, W, GE], bf16) for s in range(2)]
    same = [sb(f"same{s}", [P, T, P], bf16) for s in range(2)]
    node_id = sb("node_id", [P, G, W], f32)
    prod = [sb(f"prod1_{s}", [P, 4, J, D], f32) for s in range(2)]
    pre = [sb(f"pre{s}", [P, T, D], f32) for s in range(2)]
    msg = [sb(f"msg1_{s}", [P, T, D], f32) for s in range(2)]
    msg_res = sb("msg1_res", [P, T, D], f32)
    NP = 3 * D + 1
    parts = [sb(f"parts1_{s}", [P, T, NP + 1], bf16) for s in range(2)]

    def part_of(s, a):
        return parts[s][:, :, 0:3 * D].rearrange("p t (f a) -> p t f a", a=3)[:, :, :, a]
    total = [sb(f"total{s}", [P, T, D], f32) for s in range(2)]
    gap = [sb(f"gap{s}", [P, T], f32) for s in range(2)]
    row_f = sb("row_f", [P, T], f32)
    row = [sb(f"row{s}", [P, T], i32) for s in range(2)]
    ps_q = [ps(f"ps_q1{u}", [P, 4, J, D]) for u in range(2)]
    ps_s = [ps(f"ps_s1{s}", [P, T, 64]) for s in range(2)]
    iota_col = sb("iota_col", [P, 4 * S.LC], i16)
    src_i = sb("src_int", [P, G, WIDE], i32)
    src_col = sb("src_col", [P, G, WIDE], f32)
    src_r = sb("src_r", [P, G, WIDE], f32)
    hot_col = [sb(f"hot_col{s}", [P, WIDE, 4, S.LC], bf16) for s in range(2)]
    placed = [sb(f"placed{s}", [P, WIDE, HI * D, 3], bf16) for s in range(2)]
    acc = sb("acc_wide", [P, 4, S.LC], f32)
    ps_wide = ps("ps_wide", [P, 4, 512])

    names = ("l1_dve l1_tables hotT_ready same_ready gathered mult1 red1 silu_ready n_hi n_res n_mid n_lo "
             "summed total_ready gap_ready rowf_ready row_ready scatters_begun "
             "col_ready place_ready wide_done acc_added").split()
    q = {n: sem(n) for n in names}
    in_sems = {n: [sem(f"{n}{s}") for s in range(2)] for n in ("e8_in", "drow_in", "srow_in")}
    added = [sem(f"sum_added{t}") for t in range(TP)]
    weights_set, tables_dve, iota_set = sem("weights_set"), sem("tables_dve"), sem("iota_set")
    with ExitStack() as c_:
        first_windows(nc, S, k, sem, c_, "l1")
    with nc.Block() as block:
        @block.gpsimd
        def _(pool):
            pool.iota(iota_col[:, :], pattern=[[1, 4 * S.LC]], base=0, channel_multiplier=0).then_inc(iota_set, 1)
            pool.wait_ge(iota_set, 1)

        @block.vector
        def _(v):
            link = chain(v, tables_dve)
            v.memset(acc[:, :, :], 0.0)
            link(v.tensor_copy(src_i[:, :, :], k.src[:, :, TP:]))
            link(v.tensor_scalar(src_i[:, :, :], src_i[:, :, :], int(math.log2(HI)), None,
                                 ALU.arith_shift_right))
            link(v.tensor_copy(src_col[:, :, :], src_i[:, :, :]))
            link(v.scalar_tensor_tensor(src_r[:, :, :], src_col[:, :, :], float(-HI), k.src[:, :, TP:],
                                        ALU.mult, ALU.add))
            for s in range(2):
                v.tensor_copy(parts[s][:, :, 3 * D:NP], k.weight[:, :].unsqueeze(1).broadcast_to([P, T, 1])
                              ).then_inc(weights_set, 1)
            v.wait_ge(weights_set, 2)

    with nc.Fori(0, n_passes) as _:
        with nc.Block() as block:

            @block.sync
            def _(sp):
                def load(g, s, use):
                    e0 = min(g * GE, S.E - GE) if isinstance(g, int) else g * GE
                    need(sp, q["mult1"], (g - 1) * 2)
                    need(sp, q["hotT_ready"], g - 1)
                    need(sp, q["same_ready"], g - 1)
                    sp.dma_start(ea[s][:, :, :].rearrange("p t f -> p (t f)"),
                                 ea8[bass.ds(e0, GE), :].rearrange("(p t) f -> p (t f)", t=T)
                                 ).then_inc(in_sems["e8_in"][s], 16)
                    sp.dma_start(dst_row[s][:, :],
                                 k.dst_rows[bass.ds(g, 1), :].broadcast_to([P, GE])
                                 ).then_inc(in_sems["drow_in"][s], 16)
                    sp.dma_start(src_row[s][:, :, :].rearrange("p t f -> p (t f)"),
                                 k.src_rows[bass.ds(g, 1), :].broadcast_to([P, GE])
                                 ).then_inc(in_sems["srow_in"][s], 16)
                each(sp, G, load, tail=2)

            @block.vector
            def _(v):
                link = chain(v, q["l1_dve"])
                set_windows(v, link, S, k)
                for b in range(W):
                    link(v.tensor_scalar(node_id[:, :, b], k.win[:, :], float(b), float(P), ALU.add, ALU.mult))
                link(v.tensor_scalar(node_id[:, :, :], node_id[:, :, :], k.pidx[:, 0:1], None, ALU.add))
                v.sem_inc(q["l1_tables"], 1)

                def one_hot(g, s, use):
                    v.wait_ge(in_sems["drow_in"][s], 16 * (use + 1))
                    need(v, q["gathered"], (g - 1) * 2)
                    for b in range(W):
                        last = v.tensor_scalar(hotT[s][:, b, :], dst_row[s][:, :],
                                               node_id[:, bass.ds(g, 1), b], None, ALU.is_equal)
                    last.then_inc(q["hotT_ready"], 1)

                def same_source(g, s, use):
                    v.wait_ge(in_sems["srow_in"][s], 16 * (use + 1))
                    need(v, q["summed"], g - 1)
                    for t in range(TP):
                        last = v.tensor_scalar(same[s][:, t, :], src_row[s][:, t, :],
                                               k.src[:, bass.ds(g, 1), t:t + 1].rearrange("p g t -> p (g t)"),
                                               None, ALU.is_equal)
                    last.then_inc(q["same_ready"], 1)

                def unit(g, s, u, use):
                    n = g * 2 + u
                    if u == 0:
                        v.wait_ge(in_sems["e8_in"][s], 16 * (use + 1))
                    v.wait_ge(q["gathered"], n + 1)
                    need(v, q["red1"], n - 1)
                    v.tensor_tensor(prod[u][:, :, :, :], ps_q[u][:, :, :, :],
                                    ea[s][:, 4 * u:4 * u + 4, :].unsqueeze(3).broadcast_to([P, 4, J, D]),
                                    ALU.mult).then_inc(q["mult1"], 1)

                def sum_unit(g, s, u):
                    n = g * 2 + u
                    v.wait_ge(q["mult1"], n + 1)
                    if u == 0:
                        need(v, q["silu_ready"], g - 1)
                    v.tensor_reduce(pre[s][:, 4 * u:4 * u + 4, :],
                                    prod[u][:, :, :, :].rearrange("p t j h -> p t h j"), X,
                                    ALU.add).then_inc(q["red1"], 1)

                def residue(g, s):
                    v.wait_ge(q["n_hi"], g + 1)
                    need(v, q["n_lo"], g)
                    v.tensor_tensor(msg_res[:, :, :], msg[s][:, :, :], part_of(s, 0),
                                    ALU.subtract).then_inc(q["n_res"], 1)

                def low(g, s):
                    v.wait_ge(q["n_mid"], g + 1)
                    v.tensor_tensor(part_of(s, 2), msg_res[:, :, :], part_of(s, 1),
                                    ALU.subtract).then_inc(q["n_lo"], 1)

                def columns(g, s):
                    need(v, q["wide_done"], g - 1)
                    for w in range(WIDE):
                        last = v.tensor_scalar(hot_col[s][:, w, :, :].rearrange("p a b -> p (a b)"),
                                               iota_col[:, :], src_col[:, bass.ds(g, 1), w], None,
                                               ALU.is_equal)
                    last.then_inc(q["col_ready"], 1)

                def place(g, s):
                    need(v, q["wide_done"], g - 1)
                    v.wait_ge(q["n_lo"], g + 1)
                    for w in range(WIDE):
                        last = v.scalar_tensor_tensor(
                            placed[s][:, w, :, :].rearrange("p (r f) a -> p r (f a)", r=HI),
                            k.iota[:, 0:HI].unsqueeze(2).broadcast_to([P, HI, 3 * D]),
                            src_r[:, bass.ds(g, 1), w],
                            parts[s][:, TP + w, 0:3 * D].unsqueeze(1).broadcast_to([P, HI, 3 * D]),
                            ALU.is_equal, ALU.mult)
                    last.then_inc(q["place_ready"], 1)

                def totals(g, s, use):
                    v.wait_ge(q["summed"], g + 1)
                    for t in range(TP):
                        need(v, added[t], 16 * (g - 1))
                    v.tensor_reduce(total[s][:, 0:TP, :],
                                    ps_s[s][:, 0:TP, 0:3 * D].rearrange("p t (h a) -> p t h a", a=3), X,
                                    ALU.add).then_inc(q["total_ready"], 1)
                    v.tensor_scalar(gap[s][:, 0:TP], k.src[:, bass.ds(g, 1), 0:TP].rearrange("p g t -> p (g t)"),
                                    k.trash[:, 0:1], None, ALU.subtract).then_inc(q["gap_ready"], 1)
                    v.wait_ge(q["gap_ready"], g + 1)
                    need(v, q["row_ready"], g)
                    v.scalar_tensor_tensor(row_f[:, 0:TP], ps_s[s][:, 0:TP, 3 * D], k.weight25[:, 0:1],
                                           gap[s][:, 0:TP], ALU.is_lt, ALU.mult).then_inc(q["rowf_ready"], 1)
                    v.wait_ge(q["rowf_ready"], g + 1)
                    v.tensor_scalar(row[s][:, 0:TP], row_f[:, 0:TP], k.trash[:, 0:1], None,
                                    ALU.add).then_inc(q["row_ready"], 1)

                one_hot(0, 0, 0)
                same_source(0, 0, 0)

                def body(g, s, use):
                    ahead = not isinstance(g, int)
                    unit(g, s, 0, use)
                    if ahead or g >= 1:
                        residue(g - 1, 1 - s)
                    sum_unit(g, s, 0)
                    if ahead or g + 1 < G:
                        one_hot(g + 1, 1 - s, use if s == 0 else use + 1)
                    unit(g, s, 1, use)
                    if ahead or g >= 1:
                        low(g - 1, 1 - s)
                    sum_unit(g, s, 1)
                    if ahead or g >= 2:
                        totals(g - 2, s, use - 1)
                    if ahead or g >= 1:
                        place(g - 1, 1 - s)
                    if ahead or g + 1 < G:
                        same_source(g + 1, 1 - s, use if s == 0 else use + 1)
                    if ahead or g >= 1:
                        columns(g - 1, 1 - s)
                each(v, G, body, head=4, tail=2)
                residue(G - 1, 1)
                low(G - 1, 1)
                place(G - 1, 1)
                columns(G - 1, 1)
                totals(G - 2, 0, G // 2 - 1)
                totals(G - 1, 1, G // 2 - 1)
                v.wait_ge(q["wide_done"], G)
                v.tensor_tensor(acc[:, :, :], acc[:, :, :], ps_wide[:, :, 0:S.LC],
                                ALU.add).then_inc(q["acc_added"], 1)
                v.wait_ge(q["acc_added"], 1)

            @block.scalar
            def _(a):
                def silu(g, s):
                    a.wait_ge(q["red1"], g * 2 + 2)
                    need(a, q["n_res"], g - 1)
                    a.activation(msg[s][:, :, :], pre[s][:, :, :], ACT.Silu,
                                 scale=NORM).then_inc(q["silu_ready"], 1)

                def hi(g, s):
                    a.wait_ge(q["silu_ready"], g + 1)
                    need(a, q["summed"], g - 1)
                    a.activation(part_of(s, 0), msg[s][:, :, :], ACT.Copy).then_inc(q["n_hi"], 1)

                def mid(g, s):
                    a.wait_ge(q["n_res"], g + 1)
                    a.activation(part_of(s, 1), msg_res[:, :, :], ACT.Copy).then_inc(q["n_mid"], 1)

                def body(g, s, use):
                    silu(g, s)
                    hi(g, s)
                    mid(g, s)
                each(a, G, body, head=4)

            @block.tensor
            def _(pe):
                pe.wait_ge(q["l1_tables"], 1)

                def gather(g, s):
                    pe.wait_ge(q["hotT_ready"], g + 1)
                    at = pe.value_load(k.win_i[0:1, bass.ds(g, 1)], min_val=0, max_val=S.B)
                    for u in range(2):
                        need(pe, q["mult1"], g * 2 + u - 1)
                        for w in range(4):
                            t = 4 * u + w
                            for b in range(W):
                                for part in range(3):
                                    last = pe.matmul(
                                        ps_q[u][:, w, :, :].rearrange("p j h -> p (j h)"),
                                        hotT[s][:, b, t * P:(t + 1) * P],
                                        k.Q[:, bass.ds(at + b, 1), part, :].rearrange("p b w -> p (b w)"),
                                        start=(b == 0 and part == 0), stop=(b == W - 1 and part == 2))
                        last.then_inc(q["gathered"], 1)

                def sum_rows(g, s):
                    pe.wait_ge(q["n_lo"], g + 1)
                    pe.wait_ge(q["same_ready"], g + 1)
                    need(pe, q["rowf_ready"], g - 1)
                    for t in range(TP):
                        last = pe.matmul(ps_s[s][:, t, 0:NP], same[s][:, t, :], parts[s][:, t, 0:NP],
                                         start=True, stop=True)
                    last.then_inc(q["summed"], 1)

                def sum_wide(g, s):
                    pe.wait_ge(q["place_ready"], g + 1)
                    pe.wait_ge(q["col_ready"], g + 1)
                    for w in range(WIDE):
                        for part in range(3):
                            for a in range(4):
                                first = isinstance(g, int) and g == 0 and w == 0 and part == 0
                                last = pe.matmul(ps_wide[:, a, 0:S.LC],
                                                 placed[s][:, w, :, part],
                                                 hot_col[s][:, w, a, :], start=first,
                                                 stop=isinstance(g, int) and g == G - 1 and w == WIDE - 1
                                                 and part == 2, skip_group_check=True)
                    last.then_inc(q["wide_done"], 1)

                def body(g, s, use):
                    gather(g, s)
                    if not isinstance(g, int) or g >= 2:
                        sum_wide(g - 2, s)
                    if not isinstance(g, int) or g >= 1:
                        sum_rows(g - 1, 1 - s)
                each(pe, G, body, head=4)
                sum_rows(G - 1, 1)
                sum_wide(G - 2, 0)
                sum_wide(G - 1, 1)

            @block.gpsimd
            def _(pool):
                def scatter(g, s, use):
                    pool.wait_ge(q["row_ready"], g + 1)
                    pool.wait_ge(q["total_ready"], g + 1)
                    for t in range(TP):
                        need(pool, added[t], 16 * g)
                        pool.sem_inc(q["scatters_begun"], 1)
                        pool.indirect_dma_start(
                            k.sums[t], bass.IndirectOffsetOnAxis(ap=row[s][:, t:t + 1], axis=0),
                            total[s][:, t, :], None, compute_op=ALU.add).then_inc(added[t], 16)
                each(pool, G, scatter)
                for t in range(TP):
                    pool.wait_ge(added[t], 16 * G)
                pool.dma_reset()

        clear_all(nc, [*q.values(), *(x for r in in_sems.values() for x in r), *added])

    with ExitStack() as c_:
        turned = k.agg[:, :, :].rearrange("p b f -> p (b f)").rearrange("p (i f) -> p i f", f=P)
        chunks = [(i, min(P, S.LO - i * P)) for i in range(math.ceil(S.LO / P))]
        t_done, t_copied, t_stored = sem("wt_done"), sem("wt_copied"), sem("wt_stored")
        block = c_.enter_context(nc.Block())

        def bank(i):
            return ps_wide[:, i % 4, 0:P]

        @block.tensor
        def _(pe):
            flat = acc[:, :, :].rearrange("p a b -> p (a b)")
            for i, n in chunks:
                need(pe, t_copied, i - 3)
                pe.transpose(bank(i)[0:n, :], flat[:, i * P:i * P + n], k.ident[:, :]).then_inc(t_done, 1)

        @block.scalar
        def _(a):
            for i, n in chunks:
                a.wait_ge(t_done, i + 1)
                a.activation(turned[0:n, i, :], bank(i)[0:n, :], ACT.Copy).then_inc(t_copied, 1)

        @block.sync
        def _(sp):
            table = k.sums[T - 1][0:HI * S.LO, :].rearrange("(c r) f -> c (r f)", r=HI)
            full, (i, n) = len(chunks) - 1, chunks[-1]
            sp.wait_ge(t_copied, len(chunks))
            sp.dma_start(table[0:full * P, :].rearrange("(i p) f -> p i f", p=P),
                         turned[:, 0:full, :]).then_inc(t_stored, 16)
            sp.dma_start(table[full * P:, :], turned[0:n, i, :]).then_inc(t_stored, 16)
            sp.wait_ge(t_stored, 32)


def finish(nc, S, k, sem, c, Wupd, out):
    FP = 125
    FC = S.N * D // FP
    NLIN = float(1.0 / np.float32(np.sqrt(D)))
    NUPD = float(1.0 / np.float32(np.sqrt(D * D)))

    def sb(name, shape, dt=f32, c=c):
        return c.enter_context(nc.sbuf_tensor(name, shape, dt))
    acc = sb("acc", [FP, FC])
    bd_upd = sb("bd_upd", [P, T, D * D])
    with ExitStack() as c_:
        part = [sb(f"table{t}", [FP, FC], f32, c_) for t in range(1, T)]
        tab_in = [sem(f"tab_in{t}") for t in range(T)]
        summed, flat_out, bd_clear, bd_in = sem("tab_sum"), sem("flat_out"), sem("bdu_clear"), sem("bdu_in")
        agg_clear, agg_in = sem("agg_clear"), sem("agg_in")
        block = c_.enter_context(nc.Block())

        def flat(t):
            return t[0:S.N, :].rearrange("a b -> (a b)").rearrange("(p f) -> p f", p=FP)

        @block.sync
        def _(sp):
            for t in range(T):
                sp.dma_start(acc[:, :] if t == 0 else part[t - 1][:, :], flat(k.sums[t])).then_inc(tab_in[t], 16)
            sp.wait_ge(summed, T - 1)
            sp.dma_start(flat(k.sums_all), acc[:, :]).then_inc(flat_out, 16)
            sp.wait_ge(flat_out, 16)
            sp.wait_ge(agg_clear, 1)
            sp.dma_start(k.agg[:, 0:S.B - 1, :],
                         k.sums_all[0:P * (S.B - 1), :].rearrange("(c p) f -> p c f", p=P)).then_inc(agg_in, 16)
            sp.dma_start(k.agg[0:S.REST, S.B - 1, :], k.sums_all[P * (S.B - 1):, :]).then_inc(agg_in, 16)
            sp.wait_ge(agg_in, 32)

        @block.gpsimd
        def _(pool):
            pool.memset(bd_upd[:, :, :], 0.0).then_inc(bd_clear, 1)
            pool.memset(k.agg[:, :, :], 0.0).then_inc(agg_clear, 1)

        @block.scalar
        def _(a):
            a.wait_ge(bd_clear, 1)
            for b in range(T):
                a.dma_start(bd_upd[D * b:D * (b + 1), b, :],
                            Wupd.rearrange("i h k -> i (h k)")).then_inc(bd_in, 16)
            a.wait_ge(bd_in, 16 * T)

        @block.vector
        def _(v):
            v.wait_ge(tab_in[0], 16)
            for t in range(1, T):
                v.wait_ge(tab_in[t], 16)
                need(v, summed, t - 1)
                v.tensor_tensor(acc[:, :], acc[:, :], part[t - 1][:, :], ALU.add).then_inc(summed, 1)

    with ExitStack() as c_:
        lin = NodeLinear(nc, S, sem, c_, "lin", k.agg, k.bd_lin, D)
        block = c_.enter_context(nc.Block())

        @block.tensor
        def _(pe):
            lin.tensor(pe, k.ident[:, :])

        @block.scalar
        def _(a):
            lin.scalar(a)

        @block.vector
        def _(v):
            def body(ch, s, use):
                v.wait_ge(lin.done, ch + 1)
                v.tensor_scalar_mul(k.agg[:, bass.ds(ch * T, T), :],
                                    lin.bank(s, 0)[:, :].rearrange("p (b f) -> p b f", f=D),
                                    NLIN).then_inc(lin.taken, 1)
            each(v, S.NC, body, head=2 + S.NC % 2)

    u = sb("u", [P, S.BP, D])
    with ExitStack() as c_:
        prod = [sb(f"uprod{i}", [P, 2, D, D], f32, c_) for i in range(2)]
        upd = NodeLinear(nc, S, sem, c_, "upd", k.h, bd_upd, D * D)
        ured = sem("u_red")
        block = c_.enter_context(nc.Block())

        @block.tensor
        def _(pe):
            upd.tensor(pe, k.ident[:, :])

        @block.scalar
        def _(a):
            upd.scalar(a)

        @block.vector
        def _(v):
            def body(ch, s, use):
                for j in range(4):
                    n = ch * 4 + j
                    b0 = ch * T + 2 * j
                    v.wait_ge(upd.done, n + 1)
                    need(v, ured, n - 1)
                    v.tensor_tensor(prod[j % 2][:, :, :, :],
                                    upd.bank(s, j)[:, :].rearrange("p (b h k) -> p b h k", b=2, h=D),
                                    k.agg[:, bass.ds(b0, 2), :].unsqueeze(3).broadcast_to([P, 2, D, D]),
                                    ALU.mult).then_inc(upd.taken, 1)
                    v.wait_ge(upd.taken, n + 1)
                    v.tensor_reduce(u[:, bass.ds(b0, 2), :],
                                    prod[j % 2][:, :, :, :].rearrange("p b h k -> p b k h"), X,
                                    ALU.add).then_inc(ured, 1)
            each(v, S.NC, body, head=2 + S.NC % 2)

    with ExitStack() as c_:
        lin = NodeLinear(nc, S, sem, c_, "out", u, k.bd_out, D)
        usilu, done, stored = sem("u_silu"), sem("result_ready"), sem("result_stored")
        block = c_.enter_context(nc.Block())

        @block.tensor
        def _(pe):
            pe.wait_ge(usilu, 1)
            lin.tensor(pe, k.ident[:, :])

        @block.scalar
        def _(a):
            a.activation(u[:, :, :], u[:, :, :], ACT.Silu, scale=NUPD).then_inc(usilu, 1)
            lin.scalar(a)

        @block.vector
        def _(v):
            def body(ch, s, use):
                v.wait_ge(lin.done, ch + 1)
                xs = k.x[:, bass.ds(ch * T, T), :]
                v.scalar_tensor_tensor(xs, lin.bank(s, 0)[:, :].rearrange("p (b f) -> p b f", f=D), NLIN,
                                       xs, ALU.mult, ALU.add).then_inc(lin.taken, 1)
            each(v, S.NC, body, head=2 + S.NC % 2)
            v.wait_ge(lin.taken, S.NC)
            v.sem_inc(done, 1)

        @block.sync
        def _(sp):
            sp.wait_ge(done, 1)
            sp.dma_start(out[0:P * (S.B - 1), :].rearrange("(c p) f -> p c f", p=P),
                         k.x[:, 0:S.B - 1, :]).then_inc(stored, 16)
            sp.dma_start(out[P * (S.B - 1):, :], k.x[0:S.REST, S.B - 1, :]).then_inc(stored, 16)
            sp.wait_ge(stored, 32)


_INS = ["x", "src", "dst", "edge_attr_16", "edge_attr_8", "L0_gnn_W1", "L0_gnn_b1", "L0_gnn_W2",
        "L0_gnn_b2", "L0_gnn_root", "L0_gnn_bias", "L0_gnn_gamma", "L0_gnn_beta", "L1_gnn_W_msg_tp",
        "L1_gnn_W_msg_lin", "L1_gnn_W_upd_tp", "L1_gnn_W_upd_lin"]


def kernel(**inputs):
    import numpy as _np
    import concourse.bacc as _bacc
    from concourse import mybir as _mybir
    from concourse.bass_utils import run_bass_kernel_spmd as _run

    nc = _bacc.Bacc("TRN2", target_bir_lowering=False, num_devices=1)
    arrays, args = {}, []
    for name in _INS:
        a = _np.ascontiguousarray(inputs[name])
        arrays[f"in_{name}"] = a
        args.append(nc.dram_tensor(f"in_{name}", a.shape, _mybir.dt.from_np(a.dtype), kind="ExternalInput").ap())
    out = nc.dram_tensor("out", inputs["x"].shape, _mybir.dt.float32, kind="ExternalOutput").ap()
    build(nc, *args, out)
    r = _run(nc, [arrays], core_ids=[0])
    return r.results[0]["out"]
```

```python
import math
from contextlib import ExitStack, contextmanager

import numpy as np

import concourse.bass as bass
from concourse import mybir

P = 128
D = 16
T = 8
GE = P * T
W = 2
WIDE = 2
TP = T - WIDE
TABLES = TP + 1
HI = P // D
ACT_BLOCKS = 4
LN_EPS = 1e-5
BN_EPS = 1e-5

f32, bf16 = mybir.dt.float32, mybir.dt.bfloat16
i32, i16 = mybir.dt.int32, mybir.dt.int16
ALU = mybir.AluOpType
ACT = mybir.ActivationFunctionType
X = mybir.AxisListType.X


def need(engine, sem, count):
    if isinstance(count, int) and count <= 0:
        return
    engine.wait_ge(sem, count)


def each(engine, count, body, head=2, tail=0):
    for c in range(head):
        body(c, c % 2, c // 2)
    assert (count - head - tail) % 2 == 0
    with engine.Fori(0, (count - head - tail) // 2) as i:
        for u in range(head, head + 2):
            body(i * 2 + u, u % 2, i + u // 2)
    for c in range(count - tail, count):
        body(c, c % 2, c // 2)


def chain(engine, sem):
    count = [0]

    def link(instruction):
        count[0] += 1
        instruction.then_inc(sem, 1)
        engine.wait_ge(sem, count[0])
    return link


def clear_all(nc, sems):
    nums = [s.num for s in sems]
    nc.all_engine_barrier(sems_to_clear=range(min(nums), max(nums) + 1))


@contextmanager
def semaphores(nc):
    held = []
    with ExitStack() as c:
        def sem(name):
            held.append(c.enter_context(nc.semaphore(name)))
            return held[-1]
        yield sem
        clear_all(nc, held)


class Shapes:
    def __init__(self, n, e):
        self.N, self.E = n, e
        self.FULL = e // GE
        self.G = 2 * math.ceil((self.FULL + 1) / 2)
        self.DUP = GE - e % GE
        assert self.FULL in (self.G - 1, self.G - 2) and self.G % 4 == 0
        self.CH = 4
        self.CG = self.G // self.CH
        assert self.CG <= P
        self.B = math.ceil(n / P)
        self.REST = n - P * (self.B - 1)
        self.NC = math.ceil((self.B + W) / T)
        self.BP = T * self.NC
        self.LC = math.ceil(math.ceil(n / HI) / 4)
        self.LO = math.ceil(n / HI)
        assert self.LC <= 512 and HI * self.LO <= n + P


def build(nc, x, src, dst, ea16, ea8, W1, b1, W2, b2, root, bias, gamma, beta,
          Wmsg, Wmsg_lin, Wupd, Wupd_lin, out):
    S = Shapes(x.shape[0], src.shape[0])
    with ExitStack() as ctx:
        def sb(name, shape, dt, c=ctx):
            return c.enter_context(nc.sbuf_tensor(name, shape, dt))

        class K:
            pass
        k = K()
        k.rows = nc.dram_tensor("gather_rows", (S.N, 2 * D), f32, kind="Internal").ap()
        k.dst_rows = nc.dram_tensor("dst_rows", (S.G, GE), i16, kind="Internal").ap()
        k.src_rows = nc.dram_tensor("src_rows", (S.G, GE), i16, kind="Internal").ap()
        k.sums = [nc.dram_tensor(f"sums{t}", (S.N + P, D), f32, kind="Internal").ap()
                  for t in range(TABLES)]
        k.q_rows = nc.dram_tensor("q_rows", (P * S.BP, 3 * P), bf16, kind="Internal").ap()
        k.sums_all = nc.dram_tensor("sums_all", (S.N, D), f32, kind="Internal").ap()

        k.ident = sb("ident", [P, P], f32)
        k.identb = sb("identb", [P, P], bf16)
        k.ones = sb("ones", [P, P], f32)
        k.pidx = sb("pidx", [P, 1], f32)
        k.trash = sb("trash", [P, 1], f32)
        k.weight = sb("weight", [P, 1], f32)
        k.weight25 = sb("weight25", [P, 1], f32)
        k.iota = sb("iota", [P, W * P], bf16)
        k.valid = sb("valid", [P, S.BP], f32)
        k.zeros = sb("zeros", [P, 512], f32)
        k.W1p = sb("W1p", [96, 256], bf16)
        k.b1 = sb("b1c", [P, 2], f32)
        k.W2 = sb("W2s", [P, 2, 256], f32)
        k.bias = sb("biasb", [P, D], f32)
        k.gamma = sb("gammab", [P, D], f32)
        k.beta = sb("betab", [P, D], f32)
        k.bd_pre = sb("bd_pre", [P, T, 2 * D], f32)
        k.bd_lin = sb("bd_lin", [P, T, D], f32)
        k.bd_out = sb("bd_out", [P, T, D], f32)
        k.x = sb("xn", [P, S.BP, D], f32)
        k.h = sb("hn", [P, S.BP, D], f32)
        k.agg = sb("aggn", [P, S.BP, D], f32)
        k.dst = sb("dst_t", [P, S.G, T], f32)
        k.src = sb("src_t", [P, S.G, T], f32)
        k.first = sb("first_t", [P, S.G], f32)
        k.base = sb("base_t", [P, S.G], f32)
        k.win = sb("win_t", [P, S.G], f32)
        k.win_i = sb("win_i", [1, S.G], i32)
        k.rel = sb("rel_t", [P, S.G, T], f32)
        k.first_node = sb("first_node", [P, S.G], f32)
        k.passes = sb("passes", [P, 2], i32)

        with semaphores(nc) as sem:
            setup(nc, S, k, sem, src, dst, x, W1, b1, W2, b2, root, bias, gamma, beta)
        n_passes0 = nc.values_load(k.passes[0:1, 0:1], min_val=1, max_val=S.B // W + 1)
        n_passes1 = nc.values_load(k.passes[0:1, 1:2], min_val=1, max_val=S.B)

        with semaphores(nc) as sem, ExitStack() as c:
            pre_layer(nc, S, k, sem, c)
        with semaphores(nc) as sem, ExitStack() as c:
            layer0(nc, S, k, sem, c, ea16, n_passes0)
        with semaphores(nc) as sem, ExitStack() as c:
            k.Q = sb("Q", [P, S.BP, 3, P], bf16, c)
            between(nc, S, k, sem, c, Wmsg, Wmsg_lin, Wupd_lin)
        with semaphores(nc) as sem, ExitStack() as c:
            layer1(nc, S, k, sem, c, ea8, n_passes1)
        with semaphores(nc) as sem, ExitStack() as c:
            finish(nc, S, k, sem, c, Wupd, out)


def setup(nc, S, k, sem, src, dst, x, W1, b1, W2, b2, root, bias, gamma, beta):
    CG, CH, G = S.CG, S.CH, S.G
    with ExitStack() as c:
        def sb(name, shape, dt):
            return c.enter_context(nc.sbuf_tensor(name, shape, dt))
        raw = [[sb(f"raw{w}{i}", [CG, GE], i32) for i in range(CH)] for w in "ds"]
        flt = [[sb(f"flt{w}{i}", [CG, GE], f32) for i in range(CH)] for w in "ds"]
        perm = [[sb(f"perm{w}{i}", [CG, T, P], i16) for i in range(CH)] for w in "ds"]
        lohi = sb("lohi", [CG, CH, 2], f32)
        lohi_i = sb("lohi_i", [CG, CH, 2], i32)
        blk = sb("blk", [CG, CH, 2], f32)
        node_span = sb("node_span", [CG, CH, 1], f32)
        qrep = sb("qrep", [CG, CH, 4, P], f32)
        span = sb("span", [P, 2, G], f32)
        smax = sb("smax", [P, 2], f32)
        smax_i = sb("smax_i", [P, 2], i32)
        smax_b = sb("smax_b", [P, 2], i32)
        wint = sb("wint", [P, 1], i32)
        iota_i = sb("iota_i", [P, W * P], i32)
        pidx_i = sb("pidx_i", [P, 1], i32)
        ps_d = [c.enter_context(nc.psum_tensor(f"ps_d{i}", [P, 4, P], f32)) for i in range(2)]
        ps_s = [c.enter_context(nc.psum_tensor(f"ps_s{i}", [P, 4, P], f32)) for i in range(2)]
        ps_q = c.enter_context(nc.psum_tensor("ps_q", [P, 4, P], f32))

        idx_in = [sem(f"idx_in{i}") for i in range(CH)]
        rows_out = sem("rows_out")
        cst0, cst = sem("cst0"), sem("cst")
        dve = sem("ix_dve")
        reduced, masked = sem("reduced"), sem("masked")
        d_flt, s_flt = sem("d_flt"), sem("s_flt")
        d_perm, s_perm = sem("d_perm"), sem("s_perm")
        q_ready = sem("q_ready")
        tr_d, tr_s = sem("tr_d"), sem("tr_s")
        ev_d, ev_s = sem("ev_d"), sem("ev_s")

        nodes = NodesIn(nc, S, k, sem, c)
        block = c.enter_context(nc.Block())

        @block.sync
        def _(sp):
            sp.dma_start(nodes.w1[:, :], W1).then_inc(nodes.w_in, 16)
            for i in range(CH):
                for w, table in enumerate((dst, src)):
                    n = min(S.FULL, (i + 1) * CG) - i * CG
                    sp.dma_start(raw[w][i][0:n, :],
                                 table[i * CG * GE:(i * CG + n) * GE].rearrange("(g f) -> g f", f=GE)
                                 ).then_inc(idx_in[i], 16)
                    for r in range(n, CG):
                        sp.dma_start(raw[w][i][r:r + 1, :],
                                     table[S.E - GE:S.E].rearrange("(g f) -> g f", f=GE)
                                     ).then_inc(idx_in[i], 16)
            nodes.loads(sp, x, b1, W2, b2, root, bias, gamma, beta)
            for i in range(CH):
                sp.wait_ge(d_perm, i + 1)
                sp.dma_start(k.dst_rows[i * CG:(i + 1) * CG, :],
                             perm[0][i][:, :, :].rearrange("g t p -> g (t p)")).then_inc(rows_out, 16)
                sp.wait_ge(s_perm, i + 1)
                sp.dma_start(k.src_rows[i * CG:(i + 1) * CG, :],
                             perm[1][i][:, :, :].rearrange("g t p -> g (t p)")).then_inc(rows_out, 16)
            nodes.parts_out(sp)
            sp.wait_ge(rows_out, 32 * CH)

        def landed(i):
            n = min(S.FULL, (i + 1) * CG) - i * CG
            return 32 * (1 + CG - n)

        @block.gpsimd
        def _(pool):
            nodes.gpsimd(pool)
            pool.memset(k.ident[:, :], 0.0).then_inc(cst0, 1)
            pool.memset(k.identb[:, :], 0.0).then_inc(cst0, 1)
            pool.memset(k.ones[:, :], 1.0).then_inc(cst0, 1)
            pool.memset(k.valid[:, :], 1.0).then_inc(cst0, 1)
            pool.memset(k.zeros[:, :], 0.0).then_inc(cst0, 1)
            pool.wait_ge(cst0, 5)
            for m in (k.ident, k.identb):
                pool.affine_select(out=m[:, :], in_=m[:, :], compare_op=ALU.not_equal, fill=1.0, base=0,
                                   pattern=[[-1, P]], channel_multiplier=1).then_inc(cst, 1)
            pool.affine_select(out=k.valid[:, :], in_=k.valid[:, :], compare_op=ALU.is_ge, fill=0.0,
                               base=S.N - 1, pattern=[[-P, S.BP]], channel_multiplier=-1).then_inc(cst, 1)
            pool.iota(iota_i[:, :], pattern=[[1, W * P]], base=0, channel_multiplier=0).then_inc(cst, 1)
            pool.iota(pidx_i[:, :], pattern=[[0, 1]], base=0, channel_multiplier=1).then_inc(cst, 1)
            pool.iota(k.weight[:, :].bitcast(i32), pattern=[[0, 1]], base=(187 << 23),
                      channel_multiplier=-(1 << 23)).then_inc(cst, 1)
            pool.wait_ge(reduced, CH)
            last = flt[0][CH - 1]
            pool.affine_select(out=last[:, :], in_=last[:, :], compare_op=ALU.is_ge, fill=-1.0,
                               base=GE * (S.FULL - (CH - 1) * CG) - S.DUP, pattern=[[1, GE]],
                               channel_multiplier=-GE).then_inc(masked, 1)

        @block.vector
        def _(v):
            link = chain(v, dve)
            v.wait_ge(cst, 6)
            v.tensor_copy(k.iota[:, :], iota_i[:, :])
            link(v.tensor_copy(k.pidx[:, :], pidx_i[:, :]))
            v.tensor_scalar_add(k.trash[:, :], k.pidx[:, :], float(S.N))
            v.tensor_scalar_mul(k.weight25[:, :], k.weight[:, :], 2.5)
            nodes.vector(v)
            for i in range(CH):
                v.wait_ge(idx_in[i], landed(i))
                link(v.tensor_copy(flt[0][i][:, :], raw[0][i][:, :]))
                v.tensor_reduce(lohi[:, i, 0:1], flt[0][i][:, :], X, ALU.min)
                link(v.tensor_reduce(lohi[:, i, 1:2], flt[0][i][:, :], X, ALU.max))
                v.sem_inc(reduced, 1)
                link(v.tensor_copy(lohi_i[:, i, :], lohi[:, i, :]))
                link(v.tensor_scalar(lohi_i[:, i, :], lohi_i[:, i, :], 7, None, ALU.arith_shift_right))
                link(v.tensor_copy(blk[:, i, :], lohi_i[:, i, :]))
                v.tensor_tensor(node_span[:, i, :], lohi[:, i, 1:2], lohi[:, i, 0:1], ALU.subtract)
                link(v.tensor_tensor(blk[:, i, 1:2], blk[:, i, 1:2], blk[:, i, 0:1], ALU.subtract))
                v.tensor_scalar(qrep[:, i, 0, :], k.ones[0:CG, :], blk[:, i, 0:1], None, ALU.mult)
                v.tensor_scalar(qrep[:, i, 1, :], k.ones[0:CG, :], blk[:, i, 1:2], None, ALU.mult)
                v.tensor_scalar(qrep[:, i, 2, :], k.ones[0:CG, :], lohi[:, i, 0:1], None, ALU.mult)
                v.tensor_scalar(qrep[:, i, 3, :], k.ones[0:CG, :], node_span[:, i, :], None,
                                ALU.mult).then_inc(q_ready, 1)
                if i == CH - 1:
                    v.wait_ge(masked, 1)
                v.sem_inc(d_flt, 1)
                v.tensor_copy(perm[0][i][:, :, :],
                              flt[0][i][:, :].rearrange("g (p t) -> g t p", t=T)).then_inc(d_perm, 1)
                v.wait_ge(tr_d, i + 1)
                g0 = i * CG
                for h in range(2):
                    v.tensor_copy(k.dst[:, g0:g0 + CG, 4 * h:4 * h + 4],
                                  ps_d[h][:, :, 0:CG].rearrange("p t g -> p g t"))
                v.tensor_copy(k.first[:, g0:g0 + CG], ps_q[:, 0, 0:CG])
                v.tensor_copy(k.first_node[:, g0:g0 + CG], ps_q[:, 2, 0:CG])
                v.tensor_copy(span[:, :, g0:g0 + CG], ps_q[:, 1::2, 0:CG]).then_inc(ev_d, 1)
            v.wait_ge(ev_d, CH)
            link(v.tensor_reduce(smax[:, :], span[:, :, :], X, ALU.max))
            link(v.tensor_copy(smax_i[:, :], smax[:, :]))
            for w, bits in enumerate((1, 7)):
                link(v.tensor_scalar(smax_b[:, w:w + 1], smax_i[:, w:w + 1], bits, None,
                                     ALU.arith_shift_right))
            link(v.tensor_copy(smax[:, :], smax_b[:, :]))
            link(v.tensor_scalar_add(smax[:, :], smax[:, :], 1.0))
            link(v.tensor_copy(k.passes[:, :], smax[:, :]))

        @block.scalar
        def _(a):
            for i in range(CH):
                a.wait_ge(idx_in[i], landed(i))
                a.activation(flt[1][i][:, :], raw[1][i][:, :], ACT.Copy).then_inc(s_flt, 1)
                a.wait_ge(s_flt, i + 1)
                a.activation(perm[1][i][:, :, :], flt[1][i][:, :].rearrange("g (p t) -> g t p", t=T),
                             ACT.Copy).then_inc(s_perm, 1)
                a.wait_ge(tr_s, i + 1)
                g0 = i * CG
                for h in range(2):
                    last = a.activation(k.src[:, g0:g0 + CG, 4 * h:4 * h + 4],
                                        ps_s[h][:, :, 0:CG].rearrange("p t g -> p g t"), ACT.Copy)
                last.then_inc(ev_s, 1)

        @block.tensor
        def _(pe):
            pe.wait_ge(cst, 6)
            for i in range(CH):
                ident = k.ident[0:CG, 0:CG]
                pe.wait_ge(q_ready, i + 1)
                pe.wait_ge(d_flt, i + 1)
                need(pe, ev_d, i)
                for w in range(4):
                    pe.matmul(ps_q[:, w, 0:CG], qrep[:, i, w, :], ident, start=True, stop=True)
                for t in range(T):
                    last = pe.transpose(ps_d[t // 4][:, t % 4, 0:CG], flt[0][i][:, t::T], ident)
                last.then_inc(tr_d, 1)
                pe.wait_ge(s_flt, i + 1)
                need(pe, ev_s, i)
                for t in range(T):
                    last = pe.transpose(ps_s[t // 4][:, t % 4, 0:CG], flt[1][i][:, t::T], ident)
                last.then_inc(tr_s, 1)


class NodesIn:

    def __init__(self, nc, S, k, sem, c):
        def sb(name, shape, dt):
            return c.enter_context(nc.sbuf_tensor(name, shape, dt))
        self.S, self.k = S, k
        self.w1, self.r1, self.r2 = (sb(f"w1_{n}", [D, 256], f32) for n in ("raw", "r1", "r2"))
        self.part = [sb(f"w1part{i}", [D, 256], bf16) for i in range(3)]
        self.cleared, self.w_in, self.packed, self.dve, self.split = (
            sem(n) for n in ("cleared", "w_in", "packed", "sn_dve", "w1split"))

    def gpsimd(self, pool):
        pool.memset(self.k.x[:, self.S.B - 1:, :], 0.0).then_inc(self.cleared, 1)
        pool.memset(self.k.bd_pre[:, :, :], 0.0).then_inc(self.cleared, 1)

    def loads(self, sp, x, b1, W2, b2, root, bias, gamma, beta):
        S, k, packed = self.S, self.k, self.packed
        sp.wait_ge(self.cleared, 2)
        sp.dma_start(k.x[:, 0:S.B - 1, :],
                     x[0:P * (S.B - 1), :].rearrange("(c p) f -> p c f", p=P)).then_inc(packed, 16)
        sp.dma_start(k.x[0:S.REST, S.B - 1, :], x[P * (S.B - 1):, :]).then_inc(packed, 16)
        b2m = b2.rearrange("(i o) -> i o", o=D)
        for b in range(T):
            rows = slice(D * b, D * (b + 1))
            sp.dma_start(k.bd_pre[rows, b, 0:D], b2m).then_inc(packed, 16)
            sp.dma_start(k.bd_pre[rows, b, D:2 * D], root).then_inc(packed, 16)
        for j in range(2):
            sp.dma_start(k.b1[:, j:j + 1],
                         b1[j * P:(j + 1) * P].rearrange("(p a) -> p a", a=1)).then_inc(packed, 16)
        sp.dma_start(k.W2[:, :, :], W2.rearrange("(j p) n -> p j n", p=P)).then_inc(packed, 16)
        for t, w in ((k.bias, bias), (k.gamma, gamma), (k.beta, beta)):
            sp.dma_start(t[:, :], w.partition_broadcast(P)).then_inc(packed, 16)

    def parts_out(self, sp):
        sp.wait_ge(self.split, 1)
        for r, n in enumerate((0, 1, 2, 0, 1, 0)):
            sp.dma_start(self.k.W1p[D * r:D * (r + 1), :], self.part[n][:, :]).then_inc(self.packed, 16)
        sp.wait_ge(self.packed, 16 * (2 + 2 * T + 6 + 6))

    def vector(self, v):
        link = chain(v, self.dve)
        v.wait_ge(self.w_in, 16)
        w1, r1, r2, part = self.w1, self.r1, self.r2, self.part
        link(v.tensor_copy(part[0][:, :], w1[:, :]))
        link(v.tensor_tensor(r1[:, :], w1[:, :], part[0][:, :], ALU.subtract))
        link(v.tensor_copy(part[1][:, :], r1[:, :]))
        link(v.tensor_tensor(r2[:, :], r1[:, :], part[1][:, :], ALU.subtract))
        v.tensor_copy(part[2][:, :], r2[:, :]).then_inc(self.split, 1)


def clear_tables(engine, S, k, zeroed):
    n = S.N * D // 125
    per = [(s, min(512, n - s)) for s in range(0, n, 512)]
    for t in range(TP):
        flat = k.sums[t][0:S.N, :].rearrange("a b -> (a b)").rearrange("(p f) -> p f", p=125)
        for s, m in per:
            engine.dma_start(flat[:, s:s + m], k.zeros[0:125, 0:m]).then_inc(zeroed, 16)
        engine.dma_start(k.sums[t][S.N:, :], k.zeros[:, 0:D]).then_inc(zeroed, 16)
    engine.wait_ge(zeroed, 16 * TP * (len(per) + 1))


class Norm:

    def __init__(self, nc, S, sem, c, name):
        def sb(n, shape):
            return c.enter_context(nc.sbuf_tensor(f"{name}_{n}", shape, f32))
        self.sq = sb("sq", [P, S.BP, D])
        self.mean, self.var, self.sd = sb("mean", [P, S.BP]), sb("var", [P, S.BP]), sb("sd", [P, S.BP])
        self.shape = [P, S.BP, D]
        self.var_ready, self.sd_ready = sem(f"{name}_var"), sem(f"{name}_sd")

    def vector(self, v, link, x, h):
        def over(t):
            return t[:, :].unsqueeze(2).broadcast_to(self.shape)
        link(v.tensor_reduce(self.mean[:, :], x[:, :, :], X, ALU.add))
        link(v.tensor_scalar_mul(self.mean[:, :], self.mean[:, :], 1.0 / D))
        link(v.tensor_tensor(h[:, :, :], x[:, :, :], over(self.mean), ALU.subtract))
        link(v.tensor_tensor(self.sq[:, :, :], h[:, :, :], h[:, :, :], ALU.mult))
        link(v.tensor_reduce(self.var[:, :], self.sq[:, :, :], X, ALU.add))
        v.tensor_scalar(self.var[:, :], self.var[:, :], 1.0 / D, LN_EPS,
                        ALU.mult, ALU.add).then_inc(self.var_ready, 1)
        v.wait_ge(self.sd_ready, 1)
        link(v.reciprocal(self.sd[:, :], self.sd[:, :]))
        link(v.tensor_tensor(h[:, :, :], h[:, :, :], over(self.sd), ALU.mult))
        link(v.tensor_scalar_max(h[:, :, :], h[:, :, :], 0.0))

    def scalar(self, a):
        a.wait_ge(self.var_ready, 1)
        a.activation(self.sd[:, :], self.var[:, :], ACT.Sqrt).then_inc(self.sd_ready, 1)


class NodeLinear:

    def __init__(self, nc, S, sem, c, name, src, weights, width):
        self.S, self.k_src, self.weights, self.width = S, src, weights, width
        self.pieces = max(1, T * width // 512)
        self.cols = T * width // self.pieces
        self.xT = [c.enter_context(nc.sbuf_tensor(f"{name}_xT{i}", [P, P], f32)) for i in range(2)]
        self.ps_t = [c.enter_context(nc.psum_tensor(f"{name}_pt{i}", [P, P], f32)) for i in range(2)]
        self.ring = 2 * self.pieces if self.pieces <= 2 else self.pieces
        self.out = [c.enter_context(nc.psum_tensor(f"{name}_po{i}", [P, self.cols], f32))
                    for i in range(self.ring)]
        self.turned, self.copied = sem(f"{name}_turned"), sem(f"{name}_copied")
        self.done, self.taken = sem(f"{name}_done"), sem(f"{name}_taken")

    def bank(self, s, j):
        return self.out[s * self.pieces + j if self.pieces <= 2 else j]

    def tensor(self, pe, ident):
        def turn(c):
            need(pe, self.copied, c - 1)
            pe.transpose(self.ps_t[c % 2][:, :],
                         self.k_src[:, c * T:(c + 1) * T, :].rearrange("p b f -> p (b f)"),
                         ident).then_inc(self.turned, 1)

        def product(c):
            pe.wait_ge(self.copied, c + 1)
            w = self.weights[:, :, :].rearrange("p b w -> p (b w)")
            for j in range(self.pieces):
                need(pe, self.taken, c * self.pieces + j + 1 - self.ring)
                pe.matmul(self.bank(c % 2, j)[:, :], self.xT[c % 2][:, :],
                          w[:, j * self.cols:(j + 1) * self.cols],
                          start=True, stop=True).then_inc(self.done, 1)
        turn(0)
        for c in range(self.S.NC):
            if c + 1 < self.S.NC:
                turn(c + 1)
            product(c)

    def copy(self, a, c, s):
        a.wait_ge(self.turned, c + 1)
        need(a, self.done, (c - 1) * self.pieces)
        a.activation(self.xT[s][:, :], self.ps_t[s][:, :], ACT.Copy).then_inc(self.copied, 1)

    def scalar(self, a):
        each(a, self.S.NC, lambda c, s, use: self.copy(a, c, s), head=2 + self.S.NC % 2)


def pre_layer(nc, S, k, sem, c):
    rows = c.enter_context(nc.sbuf_tensor("rows", [P, S.BP, 2 * D], f32))
    norm = Norm(nc, S, sem, c, "ln0")
    lin = NodeLinear(nc, S, sem, c, "pre", k.h, k.bd_pre, 2 * D)
    h_ready, rows_ready, stored = sem("h0_ready"), sem("rows_ready"), sem("rows_stored")
    dve = sem("pre_dve")
    block = c.enter_context(nc.Block())

    @block.vector
    def _(v):
        link = chain(v, dve)
        norm.vector(v, link, k.x, k.h)
        v.sem_inc(h_ready, 1)
        v.tensor_copy(rows[:, :, 0:D], k.h[:, :, :])

        def body(ch, s, use):
            v.wait_ge(lin.done, ch + 1)
            y = lin.bank(s, 0)[:, :].rearrange("p (b w) -> p b w", w=2 * D)
            v.tensor_copy(rows[:, bass.ds(ch * T, T), D:2 * D], y[:, :, 0:D])
            v.tensor_tensor(k.agg[:, bass.ds(ch * T, T), :], y[:, :, D:2 * D],
                            k.bias[:, :].unsqueeze(1).broadcast_to([P, T, D]), ALU.add
                            ).then_inc(lin.taken, 1)
        each(v, S.NC, body, head=2 + S.NC % 2)
        v.wait_ge(lin.taken, S.NC)
        v.sem_inc(rows_ready, 1)

    @block.scalar
    def _(a):
        norm.scalar(a)
        lin.scalar(a)

    @block.tensor
    def _(pe):
        pe.wait_ge(h_ready, 1)
        lin.tensor(pe, k.ident[:, :])

    @block.sync
    def _(sp):
        sp.wait_ge(rows_ready, 1)
        sp.dma_start(k.rows[0:P * (S.B - 1), :].rearrange("(c p) f -> p c f", p=P),
                     rows[:, 0:S.B - 1, :]).then_inc(stored, 16)
        sp.dma_start(k.rows[P * (S.B - 1):, :], rows[0:S.REST, S.B - 1, :]).then_inc(stored, 16)
        sp.wait_ge(stored, 32)


def first_windows(nc, k, sem, c, name, first):
    block = c.enter_context(nc.Block())
    done = sem(f"{name}_first")

    @block.vector
    def _(v):
        v.tensor_copy(k.base[:, :], first[:, :]).then_inc(done, 1)
        v.wait_ge(done, 1)


def set_windows(v, link, k, last, step):
    link(v.tensor_scalar_min(k.win[:, :], k.base[:, :], float(last)))
    v.tensor_copy(k.win_i[:, :], k.win[0:1, :])
    link(v.tensor_scalar_add(k.base[:, :], k.base[:, :], float(step)))


def layer0(nc, S, k, sem, c, ea16, n_passes):
    G = S.G

    def sb(name, shape, dt):
        return c.enter_context(nc.sbuf_tensor(name, shape, dt))

    def ps(name, shape, dt=f32):
        return c.enter_context(nc.psum_tensor(name, shape, dt))

    ea = [sb(f"ea{s}", [P, T, D], f32) for s in range(2)]
    ea_parts = sb("ea_parts", [P, T, 6, D], bf16)
    ea_res = sb("ea_res", [P, T, D], f32)
    eT = [sb(f"eT{s}", [96, GE], bf16) for s in range(2)]
    hT = [sb(f"hT{s}", [P, 2, 512], f32) for s in range(2)]
    idx = [sb(f"idx{s}", [P, T], i32) for s in range(2)]
    xg = [sb(f"xg{s}", [P, T, 2 * D], f32) for s in range(2)]
    prod = [sb(f"prod{s}", [P, 2, D, D], f32) for s in range(2)]
    msg = [sb(f"msg{s}", [P, T, D], f32) for s in range(2)]
    msg_res = sb("msg_res", [P, T, D], f32)
    parts = [sb(f"parts{s}", [P, T, 3, D], bf16) for s in range(2)]
    hot = [sb(f"hot{s}", [P, T, W * P], bf16) for s in range(2)]
    win_sum = sb("win_sum", [P, W, D], f32)
    ps_e = ps("ps_e", [96, GE], bf16)
    ps_h = [ps(f"ps_h{j}", [P, 512]) for j in range(2)]
    ps_w = [ps(f"ps_w{u}", [P, 2, D, D]) for u in range(4)]
    ps_a = ps("ps_a", [P, W, 3, D])

    names = ("l0_dve ea_used e_hi e_res e_mid e_lo e_turned eT_ready hmm relued wmm multiplied "
             "reduced0 idx_ready msg_ready m_hi m_res m_mid m_lo hot_ready scattered ps_a_free added "
             "gathers_begun zeroed").split()
    q = {n: sem(n) for n in names}
    ea_in = [sem(f"ea_in{s}") for s in range(2)]
    xg_in = [[sem(f"xg_in{s}{t}") for t in range(T)] for s in range(2)]
    first_windows(nc, k, sem, c_ := ExitStack(), "l0", k.first)
    c_.close()

    with nc.Fori(0, n_passes) as _:
        with nc.Block() as block:

            @block.sync
            def _(sp):
                def load(g, s, use):
                    e0 = min(g * GE, S.E - GE) if isinstance(g, int) else sp.snap(g * GE)
                    need(sp, q["ea_used"], g - 1)
                    sp.dma_start(ea[s][:, :, :].rearrange("p t f -> p (t f)"),
                                 ea16[bass.ds(e0, GE), :].rearrange("(p t) f -> p (t f)", t=T)
                                 ).then_inc(ea_in[s], 16)
                each(sp, G, load, tail=2)
                clear_tables(sp, S, k, q["zeroed"])

            @block.gpsimd
            def _(pool):
                def gather(g, s, use):
                    pool.wait_ge(q["idx_ready"], g + 1)
                    need(pool, q["msg_ready"], g - 1)
                    pool.sem_inc(q["gathers_begun"], 1)
                    for t in range(T):
                        pool.indirect_dma_start(
                            xg[s][:, t, :], None, k.rows,
                            bass.IndirectOffsetOnAxis(ap=idx[s][:, t:t + 1], axis=0)
                        ).then_inc(xg_in[s][t], 16)
                each(pool, G, gather)
                pool.wait_ge(q["msg_ready"], G)
                pool.dma_reset()

            @block.scalar
            def _(a):
                def indices(g, s):
                    need(a, q["multiplied"], 4 * (g - 1))
                    a.activation(idx[s][:, :], k.src[:, bass.ds(g, 1), :].rearrange("p g t -> p (g t)"),
                                 ACT.Copy).then_inc(q["idx_ready"], 1)

                def edges_hi(g, s, use):
                    a.wait_ge(ea_in[s], 16 * (use + 1))
                    need(a, q["e_turned"], g)
                    a.activation(ea_parts[:, :, 0:3, :],
                                 ea[s][:, :, :].unsqueeze(2).broadcast_to([P, T, 3, D]),
                                 ACT.Copy).then_inc(q["e_hi"], 1)

                def edges_mid(g):
                    a.wait_ge(q["e_res"], g + 1)
                    a.activation(ea_parts[:, :, 3:5, :],
                                 ea_res[:, :, :].unsqueeze(2).broadcast_to([P, T, 2, D]),
                                 ACT.Copy).then_inc(q["e_mid"], 1)

                def edges_T(g, s):
                    a.wait_ge(q["e_turned"], g + 1)
                    need(a, q["hmm"], 4 * (g - 1))
                    a.activation(eT[s][:, :], ps_e[:, :], ACT.Copy).then_inc(q["eT_ready"], 1)

                def relu(c, s):
                    need(a, q["wmm"], 2 * (c - 1))
                    for j in range(2):
                        a.wait_ge(q["hmm"], 2 * c + j + 1)
                        a.activation(hT[s][:, j, :], ps_h[j][:, :], ACT.Relu,
                                     bias=k.b1[:, j:j + 1]).then_inc(q["relued"], 1)

                def msg_hi(g, s):
                    a.wait_ge(q["msg_ready"], g + 1)
                    need(a, q["scattered"], g - 1)
                    a.activation(parts[s][:, :, 0, :], msg[s][:, :, :], ACT.Copy).then_inc(q["m_hi"], 1)

                def msg_mid(g, s):
                    a.wait_ge(q["m_res"], g + 1)
                    a.activation(parts[s][:, :, 1, :], msg_res[:, :, :], ACT.Copy).then_inc(q["m_mid"], 1)

                indices(0, 0)
                edges_hi(0, 0, 0)
                edges_mid(0)
                edges_T(0, 0)
                relu(0, 0)
                edges_hi(1, 1, 0)
                edges_mid(1)

                def body(g, s, use):
                    ahead = not isinstance(g, int)
                    relu(g * 2 + 1, 1)
                    if ahead or g + 1 < G:
                        indices(g + 1, 1 - s)
                    if ahead or g >= 1:
                        msg_hi(g - 1, 1 - s)
                        msg_mid(g - 1, 1 - s)
                    if ahead or g + 1 < G:
                        edges_T(g + 1, 1 - s)
                    if ahead or g + 2 < G:
                        edges_hi(g + 2, s, use + 1)
                    if ahead or g + 1 < G:
                        relu(g * 2 + 2, 0)
                    if ahead or g + 2 < G:
                        edges_mid(g + 2)
                each(a, G, body, head=4, tail=2)
                msg_hi(G - 1, 1)
                msg_mid(G - 1, 1)

            @block.tensor
            def _(pe):
                def turn(g):
                    pe.wait_ge(q["e_lo"], g + 1)
                    need(pe, q["eT_ready"], g)
                    for t in range(T):
                        last = pe.transpose(ps_e[:, t * P:(t + 1) * P],
                                            ea_parts[:, t, :, :].rearrange("p a f -> p (a f)"),
                                            k.identb[:, :])
                    last.then_inc(q["e_turned"], 1)

                def hidden(c, g, half, s):
                    if half == 0:
                        pe.wait_ge(q["eT_ready"], g + 1)
                    for j in range(2):
                        need(pe, q["relued"], 2 * (c - 1) + j + 1)
                        pe.matmul(ps_h[j][:, :], k.W1p[:, j * P:(j + 1) * P],
                                  eT[s][:, half * 512:(half + 1) * 512],
                                  start=True, stop=True).then_inc(q["hmm"], 1)

                def edge_weights(c, half, units):
                    pe.wait_ge(q["relued"], 2 * c + 2)
                    for u in units:
                        need(pe, q["multiplied"], 2 * c + u - 3)
                        bank = ps_w[2 * half + u]
                        for w in range(2):
                            col = (2 * u + w) * P
                            for j in range(2):
                                last = pe.matmul(bank[:, w, :, :].rearrange("p i o -> p (i o)"),
                                                 hT[half][:, j, col:col + P], k.W2[:, j, :],
                                                 start=(j == 0), stop=(j == 1))
                        last.then_inc(q["wmm"], 1)

                def scatter(g, s):
                    pe.wait_ge(q["m_lo"], g + 1)
                    pe.wait_ge(q["hot_ready"], g + 1)
                    need(pe, q["ps_a_free"], g)
                    for t in range(T):
                        for b in range(W):
                            last = pe.matmul(ps_a[:, b, :, :].rearrange("p a o -> p (a o)"),
                                             hot[s][:, t, b * P:(b + 1) * P],
                                             parts[s][:, t, :, :].rearrange("p a o -> p (a o)"),
                                             start=(t == 0 and b == 0), stop=(t == T - 1),
                                             skip_group_check=True)
                    last.then_inc(q["scattered"], 1)

                turn(0)
                hidden(0, 0, 0, 0)

                def body(g, s, use):
                    more = not isinstance(g, int) or g + 1 < G
                    hidden(g * 2 + 1, g, 1, s)
                    edge_weights(g * 2, 0, (0, 1))
                    if more:
                        turn(g + 1)
                    edge_weights(g * 2 + 1, 1, (0,))
                    if more:
                        hidden(g * 2 + 2, g + 1, 0, 1 - s)
                    edge_weights(g * 2 + 1, 1, (1,))
                    if not isinstance(g, int) or g >= 1:
                        scatter(g - 1, 1 - s)
                each(pe, G, body, head=4, tail=2)
                scatter(G - 1, 1)

            @block.vector
            def _(v):
                link = chain(v, q["l0_dve"])
                set_windows(v, link, k, S.B, W)
                link(v.scalar_tensor_tensor(k.rel[:, :, :],
                                            k.win[:, :].unsqueeze(2).broadcast_to([P, G, T]), float(-P),
                                            k.dst[:, :, :], ALU.mult, ALU.add))

                def edges_res(g, s):
                    v.wait_ge(q["e_hi"], g + 1)
                    need(v, q["e_lo"], g)
                    v.tensor_tensor(ea_res[:, :, :], ea[s][:, :, :], ea_parts[:, :, 0, :],
                                    ALU.subtract).then_inc(q["e_res"], 1)
                    v.wait_ge(q["e_res"], g + 1)
                    v.sem_inc(q["ea_used"], 1)

                def edges_lo(g):
                    v.wait_ge(q["e_mid"], g + 1)
                    v.tensor_tensor(ea_parts[:, :, 5, :], ea_res[:, :, :], ea_parts[:, :, 3, :],
                                    ALU.subtract).then_inc(q["e_lo"], 1)

                def unit(g, s, u, use):
                    n = g * 4 + u
                    v.wait_ge(q["wmm"], n + 1)
                    for t in (2 * u, 2 * u + 1):
                        v.wait_ge(xg_in[s][t], 16 * (use + 1))
                    need(v, q["reduced0"], n - 1)
                    v.tensor_tensor(prod[u % 2][:, :, :, :], ps_w[u][:, :, :, :],
                                    xg[s][:, 2 * u:2 * u + 2, 0:D].unsqueeze(3).broadcast_to([P, 2, D, D]),
                                    ALU.mult).then_inc(q["multiplied"], 1)

                def sum_unit(g, s, u):
                    n = g * 4 + u
                    v.wait_ge(q["multiplied"], n + 1)
                    v.tensor_reduce(msg[s][:, 2 * u:2 * u + 2, :],
                                    prod[u % 2][:, :, :, :].rearrange("p t i o -> p t o i"), X,
                                    ALU.add).then_inc(q["reduced0"], 1)

                def add_bias(g, s):
                    v.wait_ge(q["reduced0"], g * 4 + 4)
                    v.tensor_tensor(msg[s][:, :, :], msg[s][:, :, :], xg[s][:, :, D:2 * D],
                                    ALU.add).then_inc(q["msg_ready"], 1)

                def msg_residue(g, s):
                    v.wait_ge(q["m_hi"], g + 1)
                    need(v, q["m_lo"], g)
                    v.tensor_tensor(msg_res[:, :, :], msg[s][:, :, :], parts[s][:, :, 0, :],
                                    ALU.subtract).then_inc(q["m_res"], 1)

                def msg_lo(g, s):
                    v.wait_ge(q["m_mid"], g + 1)
                    v.tensor_tensor(parts[s][:, :, 2, :], msg_res[:, :, :], parts[s][:, :, 1, :],
                                    ALU.subtract).then_inc(q["m_lo"], 1)

                def one_hot(g, s, tiles):
                    if tiles[0] == 0:
                        need(v, q["scattered"], g - 1)
                    for t in tiles:
                        last = v.tensor_scalar(hot[s][:, t, :], k.iota[:, :],
                                               k.rel[:, bass.ds(g, 1), t:t + 1].rearrange("p g t -> p (g t)"),
                                               None, ALU.is_equal)
                    if tiles[-1] == T - 1:
                        last.then_inc(q["hot_ready"], 1)

                def add_window(g):
                    v.wait_ge(q["scattered"], g + 1)
                    need(v, q["added"], g)
                    v.tensor_reduce(win_sum[:, :, :], ps_a[:, :, :, :].rearrange("p w a o -> p w o a"), X,
                                    ALU.add).then_inc(q["ps_a_free"], 1)
                    at = v.value_load(k.win_i[0:1, bass.ds(g, 1)], min_val=0, max_val=S.B)
                    v.wait_ge(q["ps_a_free"], g + 1)
                    v.tensor_tensor(k.agg[:, bass.ds(at, W), :], k.agg[:, bass.ds(at, W), :],
                                    win_sum[:, :, :], ALU.add).then_inc(q["added"], 1)

                edges_res(0, 0)
                edges_lo(0)
                edges_res(1, 1)
                edges_lo(1)

                def body(g, s, use):
                    ahead = not isinstance(g, int)
                    unit(g, s, 0, use)
                    if ahead or g >= 1:
                        msg_residue(g - 1, 1 - s)
                    sum_unit(g, s, 0)
                    if ahead or g >= 2:
                        add_window(g - 2)
                    unit(g, s, 1, use)
                    one_hot(g, s, (0, 1, 2, 3))
                    sum_unit(g, s, 1)
                    if ahead or g >= 1:
                        msg_lo(g - 1, 1 - s)
                    unit(g, s, 2, use)
                    one_hot(g, s, (4, 5, 6, 7))
                    sum_unit(g, s, 2)
                    unit(g, s, 3, use)
                    if ahead or g + 2 < G:
                        edges_res(g + 2, s)
                    sum_unit(g, s, 3)
                    add_bias(g, s)
                    if ahead or g + 2 < G:
                        edges_lo(g + 2)
                each(v, G, body, head=4, tail=2)
                msg_residue(G - 1, 1)
                msg_lo(G - 1, 1)
                add_window(G - 2)
                add_window(G - 1)
                v.wait_ge(q["added"], G)

        clear_all(nc, [*q.values(), *ea_in, *(x for r in xg_in for x in r)])


def between(nc, S, k, sem, c, Wmsg, Wmsg_lin, Wupd_lin):
    def sb(name, shape, dt=f32):
        return c.enter_context(nc.sbuf_tensor(name, shape, dt))
    bd_msg = sb("bd_msg", [P, T, P])
    t0, sums, mean, var = sb("bn_t0", [P, S.BP, D]), sb("bn_s", [P, D]), sb("bn_m", [P, D]), sb("bn_v", [P, D])
    res = [sb(f"q_res{i}", [P, 4, P]) for i in range(2)]
    ps_m = c.enter_context(nc.psum_tensor("ps_m", [P, 2, D], f32))
    norm = Norm(nc, S, sem, c, "ln1")
    lin = NodeLinear(nc, S, sem, c, "msg", k.h, bd_msg, P)
    n = {x: sem(x) for x in ("bt_dve bd_clear bd_in bn_part bn_sum bn_var bn_sd h1_ready "
                             "q_hi q_mid q_lo q_stored bdf_clear bdf_in").split()}
    block = c.enter_context(nc.Block())

    @block.gpsimd
    def _(pool):
        pool.memset(bd_msg[:, :, :], 0.0).then_inc(n["bd_clear"], 1)
        for t in (k.bd_lin, k.bd_out):
            pool.memset(t[:, :, :], 0.0).then_inc(n["bdf_clear"], 1)

    @block.sync
    def _(sp):
        sp.wait_ge(n["bd_clear"], 1)
        for b in range(T):
            sp.dma_start(bd_msg[D * b:D * (b + 1), b, :],
                         Wmsg.rearrange("i j h -> i (j h)")).then_inc(n["bd_in"], 16)
        sp.wait_ge(n["bdf_clear"], 2)
        for b in range(T):
            for t, w in ((k.bd_lin, Wmsg_lin), (k.bd_out, Wupd_lin)):
                sp.dma_start(t[D * b:D * (b + 1), b, :], w).then_inc(n["bdf_in"], 16)
        for c_ in range(S.NC):
            sp.wait_ge(n["q_lo"], 2 * (c_ + 1))
            rows = k.q_rows[c_ * T * P:(c_ + 1) * T * P, :]
            sp.dma_start(rows.rearrange("(b p) f -> p b f", p=P),
                         k.Q[:, c_ * T:(c_ + 1) * T, :, :].rearrange("p b a w -> p b (a w)")
                         ).then_inc(n["q_stored"], 16)
        sp.wait_ge(n["q_stored"], 16 * S.NC)
        sp.wait_ge(n["bdf_in"], 16 * 2 * T)

    @block.vector
    def _(v):
        link = chain(v, n["bt_dve"])
        valid = k.valid[:, :].unsqueeze(2).broadcast_to([P, S.BP, D])

        def over(t):
            return t[:, :].unsqueeze(1).broadcast_to([P, S.BP, D])
        agg = k.agg[:, :, :]
        link(v.tensor_tensor(t0[:, :, :], agg, valid, ALU.mult))
        v.tensor_reduce(sums[:, :], t0[:, :, :].rearrange("p b f -> p f b"), X, ALU.add).then_inc(n["bn_part"], 1)
        v.wait_ge(n["bn_sum"], 1)
        link(v.tensor_scalar_mul(mean[:, :], ps_m[:, 0, :], 1.0 / S.N))
        link(v.tensor_tensor(agg, agg, over(mean), ALU.subtract))
        link(v.tensor_tensor(agg, agg, valid, ALU.mult))
        link(v.tensor_tensor(t0[:, :, :], agg, agg, ALU.mult))
        v.tensor_reduce(sums[:, :], t0[:, :, :].rearrange("p b f -> p f b"), X, ALU.add).then_inc(n["bn_part"], 1)
        v.wait_ge(n["bn_sum"], 2)
        v.tensor_scalar(var[:, :], ps_m[:, 1, :], 1.0 / S.N, BN_EPS, ALU.mult, ALU.add).then_inc(n["bn_var"], 1)
        v.wait_ge(n["bn_sd"], 1)
        link(v.reciprocal(var[:, :], mean[:, :]))
        link(v.tensor_tensor(var[:, :], var[:, :], k.gamma[:, :], ALU.mult))
        link(v.tensor_tensor(agg, agg, over(var), ALU.mult))
        link(v.tensor_tensor(agg, agg, over(k.beta), ALU.add))
        link(v.tensor_scalar_max(agg, agg, 0.0))
        link(v.tensor_tensor(k.x[:, :, :], k.x[:, :, :], agg, ALU.add))
        norm.vector(v, link, k.x, k.h)
        v.sem_inc(n["h1_ready"], 1)
        link(v.tensor_tensor(k.x[:, :, :], k.x[:, :, :], k.h[:, :, :], ALU.add))

        def body(c_, s, use):
            for j in range(2):
                piece, b0 = c_ * 2 + j, c_ * T + 4 * j
                v.wait_ge(n["q_hi"], piece + 1)
                need(v, n["q_lo"], piece - 1)
                y = lin.bank(s, j)[:, :].rearrange("p (b w) -> p b w", w=P)
                v.tensor_tensor(res[j][:, :, :], y, k.Q[:, bass.ds(b0, 4), 0, :],
                                ALU.subtract).then_inc(lin.taken, 1)
            for j in range(2):
                piece, b0 = c_ * 2 + j, c_ * T + 4 * j
                v.wait_ge(n["q_mid"], piece + 1)
                v.tensor_tensor(k.Q[:, bass.ds(b0, 4), 2, :], res[j][:, :, :],
                                k.Q[:, bass.ds(b0, 4), 1, :], ALU.subtract).then_inc(n["q_lo"], 1)
        each(v, S.NC, body, head=2 + S.NC % 2)

    @block.scalar
    def _(a):
        a.wait_ge(n["bn_var"], 1)
        a.activation(mean[:, :], var[:, :], ACT.Sqrt).then_inc(n["bn_sd"], 1)
        norm.scalar(a)

        def parts(c_, s, use):
            if not isinstance(c_, int) or c_ + 1 < S.NC:
                lin.copy(a, c_ + 1, 1 - s)
            for j in range(2):
                piece, b0 = c_ * 2 + j, c_ * T + 4 * j
                a.wait_ge(lin.done, piece + 1)
                y = lin.bank(s, j)[:, :].rearrange("p (b w) -> p b w", w=P)
                a.activation(k.Q[:, bass.ds(b0, 4), 0, :], y, ACT.Copy).then_inc(n["q_hi"], 1)
            for j in range(2):
                piece, b0 = c_ * 2 + j, c_ * T + 4 * j
                a.wait_ge(lin.taken, piece + 1)
                a.activation(k.Q[:, bass.ds(b0, 4), 1, :], res[j][:, :, :], ACT.Copy).then_inc(n["q_mid"], 1)
        lin.copy(a, 0, 0)
        each(a, S.NC, parts, head=3 - S.NC % 2, tail=1)

    @block.tensor
    def _(pe):
        for r in range(2):
            pe.wait_ge(n["bn_part"], r + 1)
            pe.matmul(ps_m[:, r, :], k.ones[:, :], sums[:, :], start=True, stop=True).then_inc(n["bn_sum"], 1)
        pe.wait_ge(n["bd_in"], 16 * T)
        pe.wait_ge(n["h1_ready"], 1)
        lin.tensor(pe, k.ident[:, :])


def layer1(nc, S, k, sem, c, ea8, n_passes):
    G, J = S.G, ea8.shape[1]
    NORM = float(1.0 / np.float32(np.sqrt(D * J)))

    def sb(name, shape, dt):
        return c.enter_context(nc.sbuf_tensor(name, shape, dt))

    def ps(name, shape, dt=f32):
        return c.enter_context(nc.psum_tensor(name, shape, dt))

    ea = [sb(f"e8_{s}", [P, T, J], f32) for s in range(2)]
    dst_row = [sb(f"dst_row{s}", [P, GE], i16) for s in range(2)]
    src_row = [sb(f"src_row{s}", [P, TP, P], i16) for s in range(2)]
    hotT = [sb(f"hotT{s}", [P, GE], bf16) for s in range(2)]
    same = [sb(f"same{s}", [P, TP, P], bf16) for s in range(2)]
    q_win = [sb(f"q_win{s}", [P, 3 * P], bf16) for s in range(2)]
    node_id = sb("node_id", [P, G], f32)
    prod = [sb(f"prod1_{s}", [P, 4, J, D], f32) for s in range(2)]
    pre = [sb(f"pre{s}", [P, T, D], f32) for s in range(2)]
    msg = [sb(f"msg1_{s}", [P, T, D], f32) for s in range(2)]
    msg_res = sb("msg1_res", [P, T, D], f32)
    NP = 3 * D + 1
    parts = [sb(f"parts1_{s}", [P, T, 3 * (D + 1)], bf16) for s in range(2)]

    def part_of(s, a):
        return parts[s][:, :, :].rearrange("p t (f a) -> p t f a", a=3)[:, :, 0:D, a]
    total = [sb(f"total{s}", [P, TP, D], f32) for s in range(2)]
    gap = sb("gap", [P, G, TP], f32)
    row_f = [sb(f"row_f{s}", [P, TP], f32) for s in range(2)]
    row = [sb(f"row{s}", [P, TP], i32) for s in range(2)]
    ps_q = [ps(f"ps_q1{u}", [P, 4, J, D]) for u in range(2)]
    ps_s = [ps(f"ps_s1{s}", [P, T, 64]) for s in range(2)]
    iota_col = sb("iota_col", [P, 4 * S.LC], i16)
    src_i = sb("src_int", [P, G, WIDE], i32)
    src_col = sb("src_col", [P, G, WIDE], f32)
    minus_col = sb("minus_col", [P, G, WIDE], f32)
    square = sb("square", [P, ACT_BLOCKS * S.LC], bf16)
    src_r = sb("src_r", [P, G, WIDE], f32)
    mask_r = sb("mask_r", [P, WIDE, HI], bf16)
    hot_col = [sb(f"hot_col{s}", [P, WIDE, 4, S.LC], bf16) for s in range(2)]
    placed = [sb(f"placed{s}", [P, WIDE, HI * D, 3], bf16) for s in range(2)]
    acc = sb("acc_wide", [P, 4, S.LC], f32)
    ps_wide = ps("ps_wide", [P, 4, 512])

    names = ("l1_dve l1_tables hotT_ready same_ready gathered mult1 red1 silu_ready n_hi n_res n_mid n_lo "
             "summed total_ready rowf_ready row_ready scatters_begun "
             "mask_ready col_ready squared col_ready_act place_ready wide_done acc_added").split()
    q = {n: sem(n) for n in names}
    in_sems = {n: [sem(f"{n}{s}") for s in range(2)] for n in ("e8_in", "drow_in", "srow_in", "win_in")}
    added = [sem(f"sum_added{t}") for t in range(TP)]
    weights_set, tables_dve, iota_set = sem("weights_set"), sem("tables_dve"), sem("iota_set")
    with ExitStack() as c_:
        first_windows(nc, k, sem, c_, "l1", k.first_node)
    with nc.Block() as block:
        @block.gpsimd
        def _(pool):
            pool.iota(iota_col[:, :], pattern=[[1, 4 * S.LC]], base=0, channel_multiplier=0).then_inc(iota_set, 1)
            pool.wait_ge(iota_set, 1)

        @block.vector
        def _(v):
            link = chain(v, tables_dve)
            v.memset(acc[:, :, :], 0.0)
            v.tensor_scalar(gap[:, :, :], k.src[:, :, 0:TP], k.trash[:, 0:1], None, ALU.subtract)
            link(v.tensor_copy(src_i[:, :, :], k.src[:, :, TP:]))
            link(v.tensor_scalar(src_i[:, :, :], src_i[:, :, :], int(math.log2(HI)), None,
                                 ALU.arith_shift_right))
            link(v.tensor_copy(src_col[:, :, :], src_i[:, :, :]))
            v.tensor_scalar_mul(minus_col[:, :, :], src_col[:, :, :], -1.0)
            link(v.scalar_tensor_tensor(src_r[:, :, :], src_col[:, :, :], float(-HI), k.src[:, :, TP:],
                                        ALU.mult, ALU.add))
            for s in range(2):
                v.tensor_copy(parts[s][:, :, 3 * D:NP], k.weight[:, :].unsqueeze(1).broadcast_to([P, T, 1])
                              ).then_inc(weights_set, 1)
            v.wait_ge(weights_set, 2)

    with nc.Fori(0, n_passes) as _:
        with nc.Block() as block:

            @block.sync
            def _(sp):
                sp.wait_ge(q["l1_tables"], 1)

                def load(g, s, use):
                    e0 = min(g * GE, S.E - GE) if isinstance(g, int) else g * GE
                    need(sp, q["mult1"], (g - 1) * 2)
                    need(sp, q["hotT_ready"], g - 1)
                    need(sp, q["same_ready"], g - 1)
                    need(sp, q["gathered"], (g - 1) * 2)
                    at = sp.value_load(k.win_i[0:1, bass.ds(g, 1)], min_val=0, max_val=P * (S.BP - 1))
                    sp.dma_start(q_win[s][:, :], k.q_rows[bass.ds(at, P), :]
                                 ).then_inc(in_sems["win_in"][s], 16)
                    sp.dma_start(ea[s][:, :, :].rearrange("p t f -> p (t f)"),
                                 ea8[bass.ds(e0, GE), :].rearrange("(p t) f -> p (t f)", t=T)
                                 ).then_inc(in_sems["e8_in"][s], 16)
                    sp.dma_start(dst_row[s][:, :],
                                 k.dst_rows[bass.ds(g, 1), :].broadcast_to([P, GE])
                                 ).then_inc(in_sems["drow_in"][s], 16)
                    sp.dma_start(src_row[s][:, :, :].rearrange("p t f -> p (t f)"),
                                 k.src_rows[bass.ds(g, 1), 0:TP * P].broadcast_to([P, TP * P])
                                 ).then_inc(in_sems["srow_in"][s], 16)
                each(sp, G, load, tail=2)

            @block.vector
            def _(v):
                link = chain(v, q["l1_dve"])
                set_windows(v, link, k, P * (S.BP - 1), P)
                link(v.tensor_scalar(node_id[:, :], k.win[:, :], k.pidx[:, 0:1], None, ALU.add))
                v.sem_inc(q["l1_tables"], 1)

                def one_hot(g, s, use):
                    v.wait_ge(in_sems["drow_in"][s], 16 * (use + 1))
                    need(v, q["gathered"], (g - 1) * 2)
                    v.tensor_scalar(hotT[s][:, :], dst_row[s][:, :], node_id[:, bass.ds(g, 1)], None,
                                    ALU.is_equal).then_inc(q["hotT_ready"], 1)

                def same_source(g, s, use):
                    v.wait_ge(in_sems["srow_in"][s], 16 * (use + 1))
                    need(v, q["summed"], g - 1)
                    for t in range(TP):
                        last = v.tensor_scalar(same[s][:, t, :], src_row[s][:, t, :],
                                               k.src[:, bass.ds(g, 1), t:t + 1].rearrange("p g t -> p (g t)"),
                                               None, ALU.is_equal)
                    last.then_inc(q["same_ready"], 1)

                def unit(g, s, u, use):
                    n = g * 2 + u
                    if u == 0:
                        v.wait_ge(in_sems["e8_in"][s], 16 * (use + 1))
                    v.wait_ge(q["gathered"], n + 1)
                    need(v, q["red1"], n - 1)
                    v.tensor_tensor(prod[u][:, :, :, :], ps_q[u][:, :, :, :],
                                    ea[s][:, 4 * u:4 * u + 4, :].unsqueeze(3).broadcast_to([P, 4, J, D]),
                                    ALU.mult).then_inc(q["mult1"], 1)

                def sum_unit(g, s, u):
                    n = g * 2 + u
                    v.wait_ge(q["mult1"], n + 1)
                    if u == 0:
                        need(v, q["silu_ready"], g - 1)
                    v.tensor_reduce(pre[s][:, 4 * u:4 * u + 4, :],
                                    prod[u][:, :, :, :].rearrange("p t j h -> p t h j"), X,
                                    ALU.add).then_inc(q["red1"], 1)

                def residue(g, s):
                    v.wait_ge(q["n_hi"], g + 1)
                    need(v, q["n_lo"], g)
                    v.tensor_tensor(msg_res[:, :, :], msg[s][:, :, :], part_of(s, 0),
                                    ALU.subtract).then_inc(q["n_res"], 1)

                def low(g, s):
                    v.wait_ge(q["n_mid"], g + 1)
                    v.tensor_tensor(part_of(s, 2), msg_res[:, :, :], part_of(s, 1),
                                    ALU.subtract).then_inc(q["n_lo"], 1)

                def columns(g, s):
                    need(v, q["wide_done"], g - 1)
                    for w in range(WIDE):
                        n = min(4, 4 * WIDE - ACT_BLOCKS - 4 * w)
                        if n > 0:
                            last = v.tensor_scalar(
                                hot_col[s][:, w, 0:n, :].rearrange("p a b -> p (a b)"),
                                iota_col[:, 0:n * S.LC], src_col[:, bass.ds(g, 1), w], None, ALU.is_equal)
                    last.then_inc(q["col_ready"], 1)

                def place(g, s):
                    need(v, q["wide_done"], g - 1)
                    v.wait_ge(q["n_lo"], g + 1)
                    v.tensor_tensor(mask_r[:, :, :], k.iota[:, 0:HI].unsqueeze(1).broadcast_to([P, WIDE, HI]),
                                    src_r[:, bass.ds(g, 1), :].rearrange("p g w -> p (g w)")
                                    .unsqueeze(2).broadcast_to([P, WIDE, HI]), ALU.is_equal
                                    ).then_inc(q["mask_ready"], 1)
                    v.wait_ge(q["mask_ready"], g + 1)
                    last = v.tensor_tensor(
                        placed[s][:, :, :, :].rearrange("p w (r f) a -> p w r (f a)", r=HI),
                        mask_r[:, :, :].unsqueeze(3).broadcast_to([P, WIDE, HI, 3 * D]),
                        parts[s][:, TP:, 0:3 * D].unsqueeze(2).broadcast_to([P, WIDE, HI, 3 * D]), ALU.mult)
                    last.then_inc(q["place_ready"], 1)

                def rows_to(g, s):
                    v.wait_ge(q["summed"], g + 1)
                    need(v, q["row_ready"], g - 1)
                    v.scalar_tensor_tensor(row_f[s][:, :], ps_s[s][:, 0:TP, D], k.weight25[:, 0:1],
                                           gap[:, bass.ds(g, 1), :].rearrange("p g t -> p (g t)"),
                                           ALU.is_lt, ALU.mult).then_inc(q["rowf_ready"], 1)

                one_hot(0, 0, 0)
                same_source(0, 0, 0)

                def body(g, s, use):
                    ahead = not isinstance(g, int)
                    unit(g, s, 0, use)
                    if ahead or g >= 1:
                        residue(g - 1, 1 - s)
                    sum_unit(g, s, 0)
                    if ahead or g + 1 < G:
                        one_hot(g + 1, 1 - s, use if s == 0 else use + 1)
                    unit(g, s, 1, use)
                    if ahead or g >= 1:
                        low(g - 1, 1 - s)
                    sum_unit(g, s, 1)
                    if ahead or g >= 2:
                        rows_to(g - 2, s)
                    if ahead or g >= 1:
                        place(g - 1, 1 - s)
                    if ahead or g >= 1:
                        columns(g - 1, 1 - s)
                    if ahead or g + 1 < G:
                        same_source(g + 1, 1 - s, use if s == 0 else use + 1)
                each(v, G, body, head=4, tail=2)
                residue(G - 1, 1)
                low(G - 1, 1)
                place(G - 1, 1)
                columns(G - 1, 1)
                rows_to(G - 2, 0)
                rows_to(G - 1, 1)
                v.wait_ge(q["wide_done"], G)
                v.tensor_tensor(acc[:, :, :], acc[:, :, :], ps_wide[:, :, 0:S.LC],
                                ALU.add).then_inc(q["acc_added"], 1)
                v.wait_ge(q["acc_added"], 1)

            @block.scalar
            def _(a):
                def silu(g, s):
                    a.wait_ge(q["red1"], g * 2 + 2)
                    need(a, q["n_res"], g - 1)
                    a.activation(msg[s][:, :, :], pre[s][:, :, :], ACT.Silu,
                                 scale=NORM).then_inc(q["silu_ready"], 1)

                def hi(g, s):
                    a.wait_ge(q["silu_ready"], g + 1)
                    need(a, q["summed"], g - 1)
                    a.activation(part_of(s, 0), msg[s][:, :, :], ACT.Copy).then_inc(q["n_hi"], 1)

                def mid(g, s):
                    a.wait_ge(q["n_res"], g + 1)
                    a.activation(part_of(s, 1), msg_res[:, :, :], ACT.Copy).then_inc(q["n_mid"], 1)

                def total_out(g, s):
                    a.wait_ge(q["rowf_ready"], g + 1)
                    for t in range(TP):
                        need(a, added[t], 16 * (g - 1))
                    a.activation(total[s][:, :, :], ps_s[s][:, 0:TP, 0:D], ACT.Copy
                                 ).then_inc(q["total_ready"], 1)

                def rows_out(g, s):
                    a.activation(row[s][:, :], row_f[s][:, :], ACT.Identity, bias=k.trash[:, 0:1]
                                 ).then_inc(q["row_ready"], 1)

                def columns(g, s):
                    need(a, q["wide_done"], g - 1)
                    n = 0
                    spans = []
                    for w in range(WIDE):
                        first = max(0, 4 * WIDE - ACT_BLOCKS - 4 * w)
                        if first < 4:
                            spans.append((w, first, n, (4 - first) * S.LC))
                            n += (4 - first) * S.LC
                    need(a, q["col_ready_act"], len(spans) * g)
                    for w, first, at, m in spans:
                        a.activation(square[:, at:at + m], iota_col[:, first * S.LC:], ACT.Square,
                                     bias=minus_col[:, bass.ds(g, 1), w]).then_inc(q["squared"], 1)
                    for i, (w, first, at, m) in enumerate(spans):
                        a.wait_ge(q["squared"], len(spans) * g + i + 1)
                        a.activation(hot_col[s][:, w, first:, :].rearrange("p a b -> p (a b)"),
                                     square[:, at:at + m], ACT.Relu, bias=k.ones[:, 0:1], scale=-1.0
                                     ).then_inc(q["col_ready_act"], 1)

                def body(g, s, use):
                    silu(g, s)
                    hi(g, s)
                    mid(g, s)
                    if not isinstance(g, int) or g >= 2:
                        total_out(g - 2, s)
                        rows_out(g - 2, s)
                    columns(g, s)
                each(a, G, body, head=4)
                total_out(G - 2, 0)
                rows_out(G - 2, 0)
                total_out(G - 1, 1)
                rows_out(G - 1, 1)

            @block.tensor
            def _(pe):
                pe.wait_ge(q["l1_tables"], 1)

                def gather(g, s, use):
                    pe.wait_ge(q["hotT_ready"], g + 1)
                    pe.wait_ge(in_sems["win_in"][s], 16 * (use + 1))
                    for u in range(2):
                        need(pe, q["mult1"], g * 2 + u - 1)
                        for w in range(4):
                            t = 4 * u + w
                            for part in range(3):
                                last = pe.matmul(ps_q[u][:, w, :, :].rearrange("p j h -> p (j h)"),
                                                 hotT[s][:, t * P:(t + 1) * P],
                                                 q_win[s][:, part * P:(part + 1) * P],
                                                 start=(part == 0), stop=(part == 2))
                        last.then_inc(q["gathered"], 1)

                def sum_rows(g, s):
                    pe.wait_ge(q["n_lo"], g + 1)
                    pe.wait_ge(q["same_ready"], g + 1)
                    need(pe, q["total_ready"], g - 1)
                    for t in range(TP):
                        for part in range(3):
                            n = D + 1 if part == 0 else D
                            last = pe.matmul(ps_s[s][:, t, 0:n], same[s][:, t, :],
                                             parts[s][:, t, :].rearrange("p (f a) -> p f a", a=3)[:, 0:n, part],
                                             start=(part == 0), stop=(part == 2), skip_group_check=True)
                    last.then_inc(q["summed"], 1)

                def sum_wide(g, s):
                    pe.wait_ge(q["place_ready"], g + 1)
                    pe.wait_ge(q["col_ready"], g + 1)
                    pe.wait_ge(q["col_ready_act"], (1 if ACT_BLOCKS <= 4 else 2) * (g + 1))
                    for w in range(WIDE):
                        for part in range(3):
                            for a in range(4):
                                first = isinstance(g, int) and g == 0 and w == 0 and part == 0
                                last = pe.matmul(ps_wide[:, a, 0:S.LC],
                                                 placed[s][:, w, :, part],
                                                 hot_col[s][:, w, a, :], start=first,
                                                 stop=isinstance(g, int) and g == G - 1 and w == WIDE - 1
                                                 and part == 2, skip_group_check=True)
                    last.then_inc(q["wide_done"], 1)

                def body(g, s, use):
                    gather(g, s, use)
                    if not isinstance(g, int) or g >= 2:
                        sum_wide(g - 2, s)
                    if not isinstance(g, int) or g >= 1:
                        sum_rows(g - 1, 1 - s)
                each(pe, G, body, head=4)
                sum_rows(G - 1, 1)
                sum_wide(G - 2, 0)
                sum_wide(G - 1, 1)

            @block.gpsimd
            def _(pool):
                def scatter(g, s, use):
                    pool.wait_ge(q["row_ready"], g + 1)
                    pool.wait_ge(q["total_ready"], g + 1)
                    for t in range(TP):
                        need(pool, added[t], 16 * g)
                        pool.sem_inc(q["scatters_begun"], 1)
                        pool.indirect_dma_start(
                            k.sums[t], bass.IndirectOffsetOnAxis(ap=row[s][:, t:t + 1], axis=0),
                            total[s][:, t, :], None, compute_op=ALU.add).then_inc(added[t], 16)
                each(pool, G, scatter)
                for t in range(TP):
                    pool.wait_ge(added[t], 16 * G)
                pool.dma_reset()

        clear_all(nc, [*q.values(), *(x for r in in_sems.values() for x in r), *added])

    with ExitStack() as c_:
        turned = k.agg[:, :, :].rearrange("p b f -> p (b f)").rearrange("p (i f) -> p i f", f=P)
        chunks = [(i, min(P, S.LO - i * P)) for i in range(math.ceil(S.LO / P))]
        t_done, t_copied, t_stored = sem("wt_done"), sem("wt_copied"), sem("wt_stored")
        block = c_.enter_context(nc.Block())

        def bank(i):
            return ps_wide[:, i % 4, 0:P]

        @block.tensor
        def _(pe):
            flat = acc[:, :, :].rearrange("p a b -> p (a b)")
            for i, n in chunks:
                need(pe, t_copied, i - 3)
                pe.transpose(bank(i)[0:n, :], flat[:, i * P:i * P + n], k.ident[:, :]).then_inc(t_done, 1)

        @block.scalar
        def _(a):
            for i, n in chunks:
                a.wait_ge(t_done, i + 1)
                a.activation(turned[0:n, i, :], bank(i)[0:n, :], ACT.Copy).then_inc(t_copied, 1)

        @block.sync
        def _(sp):
            table = k.sums[TP][0:HI * S.LO, :].rearrange("(c r) f -> c (r f)", r=HI)
            full, (i, n) = len(chunks) - 1, chunks[-1]
            sp.wait_ge(t_copied, len(chunks))
            sp.dma_start(table[0:full * P, :].rearrange("(i p) f -> p i f", p=P),
                         turned[:, 0:full, :]).then_inc(t_stored, 16)
            sp.dma_start(table[full * P:, :], turned[0:n, i, :]).then_inc(t_stored, 16)
            sp.wait_ge(t_stored, 32)


def finish(nc, S, k, sem, c, Wupd, out):
    FP = 125
    FC = S.N * D // FP
    NLIN = float(1.0 / np.float32(np.sqrt(D)))
    NUPD = float(1.0 / np.float32(np.sqrt(D * D)))

    def sb(name, shape, dt=f32, c=c):
        return c.enter_context(nc.sbuf_tensor(name, shape, dt))
    acc = sb("acc", [FP, FC])
    bd_upd = sb("bd_upd", [P, T, D * D])
    with ExitStack() as c_:
        part = [sb(f"table{t}", [FP, FC], f32, c_) for t in range(1, TABLES)]
        tab_in = [sem(f"tab_in{t}") for t in range(TABLES)]
        summed, flat_out, bd_clear, bd_in = sem("tab_sum"), sem("flat_out"), sem("bdu_clear"), sem("bdu_in")
        agg_clear, agg_in = sem("agg_clear"), sem("agg_in")
        block = c_.enter_context(nc.Block())

        def flat(t):
            return t[0:S.N, :].rearrange("a b -> (a b)").rearrange("(p f) -> p f", p=FP)

        @block.sync
        def _(sp):
            for t in range(TABLES):
                sp.dma_start(acc[:, :] if t == 0 else part[t - 1][:, :], flat(k.sums[t])).then_inc(tab_in[t], 16)
            sp.wait_ge(summed, TABLES - 1)
            sp.dma_start(flat(k.sums_all), acc[:, :]).then_inc(flat_out, 16)
            sp.wait_ge(flat_out, 16)
            sp.wait_ge(agg_clear, 1)
            sp.dma_start(k.agg[:, 0:S.B - 1, :],
                         k.sums_all[0:P * (S.B - 1), :].rearrange("(c p) f -> p c f", p=P)).then_inc(agg_in, 16)
            sp.dma_start(k.agg[0:S.REST, S.B - 1, :], k.sums_all[P * (S.B - 1):, :]).then_inc(agg_in, 16)
            sp.wait_ge(agg_in, 32)

        @block.gpsimd
        def _(pool):
            pool.memset(bd_upd[:, :, :], 0.0).then_inc(bd_clear, 1)
            pool.memset(k.agg[:, :, :], 0.0).then_inc(agg_clear, 1)

        @block.scalar
        def _(a):
            a.wait_ge(bd_clear, 1)
            for b in range(T):
                a.dma_start(bd_upd[D * b:D * (b + 1), b, :],
                            Wupd.rearrange("i h k -> i (h k)")).then_inc(bd_in, 16)
            a.wait_ge(bd_in, 16 * T)

        @block.vector
        def _(v):
            v.wait_ge(tab_in[0], 16)
            for t in range(1, TABLES):
                v.wait_ge(tab_in[t], 16)
                need(v, summed, t - 1)
                v.tensor_tensor(acc[:, :], acc[:, :], part[t - 1][:, :], ALU.add).then_inc(summed, 1)

    with ExitStack() as c_:
        lin = NodeLinear(nc, S, sem, c_, "lin", k.agg, k.bd_lin, D)
        block = c_.enter_context(nc.Block())

        @block.tensor
        def _(pe):
            lin.tensor(pe, k.ident[:, :])

        @block.scalar
        def _(a):
            lin.scalar(a)

        @block.vector
        def _(v):
            def body(ch, s, use):
                v.wait_ge(lin.done, ch + 1)
                v.tensor_scalar_mul(k.agg[:, bass.ds(ch * T, T), :],
                                    lin.bank(s, 0)[:, :].rearrange("p (b f) -> p b f", f=D),
                                    NLIN).then_inc(lin.taken, 1)
            each(v, S.NC, body, head=2 + S.NC % 2)

    u = sb("u", [P, S.BP, D])
    with ExitStack() as c_:
        prod = [sb(f"uprod{i}", [P, 2, D, D], f32, c_) for i in range(2)]
        upd = NodeLinear(nc, S, sem, c_, "upd", k.h, bd_upd, D * D)
        ured = sem("u_red")
        block = c_.enter_context(nc.Block())

        @block.tensor
        def _(pe):
            upd.tensor(pe, k.ident[:, :])

        @block.scalar
        def _(a):
            upd.scalar(a)

        @block.vector
        def _(v):
            def body(ch, s, use):
                for j in range(4):
                    n = ch * 4 + j
                    b0 = ch * T + 2 * j
                    v.wait_ge(upd.done, n + 1)
                    need(v, ured, n - 1)
                    v.tensor_tensor(prod[j % 2][:, :, :, :],
                                    upd.bank(s, j)[:, :].rearrange("p (b h k) -> p b h k", b=2, h=D),
                                    k.agg[:, bass.ds(b0, 2), :].unsqueeze(3).broadcast_to([P, 2, D, D]),
                                    ALU.mult).then_inc(upd.taken, 1)
                    v.wait_ge(upd.taken, n + 1)
                    v.tensor_reduce(u[:, bass.ds(b0, 2), :],
                                    prod[j % 2][:, :, :, :].rearrange("p b h k -> p b k h"), X,
                                    ALU.add).then_inc(ured, 1)
            each(v, S.NC, body, head=2 + S.NC % 2)

    with ExitStack() as c_:
        lin = NodeLinear(nc, S, sem, c_, "out", u, k.bd_out, D)
        usilu, done, stored = sem("u_silu"), sem("result_ready"), sem("result_stored")
        block = c_.enter_context(nc.Block())

        @block.tensor
        def _(pe):
            pe.wait_ge(usilu, 1)
            lin.tensor(pe, k.ident[:, :])

        @block.scalar
        def _(a):
            a.activation(u[:, :, :], u[:, :, :], ACT.Silu, scale=NUPD).then_inc(usilu, 1)
            lin.scalar(a)

        @block.vector
        def _(v):
            def body(ch, s, use):
                v.wait_ge(lin.done, ch + 1)
                xs = k.x[:, bass.ds(ch * T, T), :]
                v.scalar_tensor_tensor(xs, lin.bank(s, 0)[:, :].rearrange("p (b f) -> p b f", f=D), NLIN,
                                       xs, ALU.mult, ALU.add).then_inc(lin.taken, 1)
            each(v, S.NC, body, head=2 + S.NC % 2)
            v.wait_ge(lin.taken, S.NC)
            v.sem_inc(done, 1)

        @block.sync
        def _(sp):
            sp.wait_ge(done, 1)
            sp.dma_start(out[0:P * (S.B - 1), :].rearrange("(c p) f -> p c f", p=P),
                         k.x[:, 0:S.B - 1, :]).then_inc(stored, 16)
            sp.dma_start(out[P * (S.B - 1):, :], k.x[0:S.REST, S.B - 1, :]).then_inc(stored, 16)
            sp.wait_ge(stored, 32)


_INS = ["x", "src", "dst", "edge_attr_16", "edge_attr_8", "L0_gnn_W1", "L0_gnn_b1", "L0_gnn_W2",
        "L0_gnn_b2", "L0_gnn_root", "L0_gnn_bias", "L0_gnn_gamma", "L0_gnn_beta", "L1_gnn_W_msg_tp",
        "L1_gnn_W_msg_lin", "L1_gnn_W_upd_tp", "L1_gnn_W_upd_lin"]


def kernel(**inputs):
    import numpy as _np
    import concourse.bacc as _bacc
    from concourse import mybir as _mybir
    from concourse.bass_utils import run_bass_kernel_spmd as _run

    nc = _bacc.Bacc("TRN2", target_bir_lowering=False, num_devices=1)
    arrays, args = {}, []
    for name in _INS:
        a = _np.ascontiguousarray(inputs[name])
        arrays[f"in_{name}"] = a
        args.append(nc.dram_tensor(f"in_{name}", a.shape, _mybir.dt.from_np(a.dtype), kind="ExternalInput").ap())
    out = nc.dram_tensor("out", inputs["x"].shape, _mybir.dt.float32, kind="ExternalOutput").ap()
    build(nc, *args, out)
    r = _run(nc, [arrays], core_ids=[0])
    return r.results[0]["out"]
```
